# Optimizing a Trainium2 kernel written in Bass

```python
import numpy as np
import jax
import jax.numpy as jnp

def _softmax(x, axis=-1):
    return jax.nn.softmax(x, axis=axis)

def _gelu(x):
    return jax.nn.gelu(x, approximate=True)

def _silu(x):
    return jax.nn.silu(x)

def _sigmoid(x):
    return jax.nn.sigmoid(x)

def _layernorm(x, axis=-1, eps=1e-05):
    m = jnp.mean(x, axis=axis, keepdims=True)
    v = jnp.var(x, axis=axis, keepdims=True)
    return (x - m) / jnp.sqrt(v + eps)

def _scatter_add(tgt, idx, src, axis=0):
    return tgt.at[idx].add(src)

def _segment_sum(src, seg, n):
    return jax.ops.segment_sum(src, seg, n)
kernel_name = 'mk_adj_resnorm_d2_adj_r2_fb0e44'

def setup_inputs(seed: int=0):
    np.random.seed(seed)
    _w = jnp.asarray

    def _rec_inputs():
        import jax
        import jax.numpy as jnp
        _gk = jax.random.key(seed)
        x = -0.0002928 + 1 * jax.random.normal(jax.random.fold_in(_gk, 1), (32, 256, 256), jnp.float32)
        _w = (1.0 + jnp.arange(256, dtype=jnp.float32)) ** (-0.5)
        _w = _w / _w.mean()
        _pij = jnp.clip(0.015625 * _w[:, None] * _w[None, :], 0.0, 1.0)
        _a = jax.random.uniform(jax.random.fold_in(_gk, 2), (32, 256, 256)) < _pij
        _a = jnp.logical_or(_a, jnp.swapaxes(_a, -1, -2))
        _a = jnp.logical_or(_a, jnp.eye(256, dtype=bool))
        _af = _a.astype(jnp.float32)
        _af = _af * jax.random.uniform(jax.random.fold_in(_gk, 3), (32, 256, 256), jnp.float32, 0.05, 1)
        adj = _af
        return (x, adj)
    x, adj = _rec_inputs()

    def _L0_gnn_setup():
        import jax, jax.numpy as jnp
        import numpy as np
        B, N, DIN, DOUT, K = (4, 1024, 256, 256, 3)
        key = jax.random.key(seed)
        ks = jax.random.split(key, 8)
        X = jax.random.normal(ks[0], (B, N, DIN), dtype=jnp.float32)
        A = jax.random.uniform(ks[1], (B, N, N), dtype=jnp.float32)
        Wv = jax.random.normal(ks[2], (DIN, DOUT), dtype=jnp.float32) * 0.02
        bv = jax.random.normal(ks[3], (DOUT,), dtype=jnp.float32) * 0.02
        aw = jax.random.normal(ks[4], (2 * DOUT, 1), dtype=jnp.float32) * 0.05
        ab = jax.random.normal(ks[5], (1,), dtype=jnp.float32) * 0.05
        Wk = jax.random.normal(ks[6], (K, DIN, DOUT), dtype=jnp.float32) * 0.02
        bk = jax.random.normal(ks[7], (K, DOUT), dtype=jnp.float32) * 0.02
        return {'X': X, 'A': A, 'Wv': Wv, 'bv': bv, 'aw': aw, 'ab': ab, 'Wk': Wk, 'bk': bk}
    _L0_gnn_all = _L0_gnn_setup()
    _L0_gnn_in = {k: v for k, v in _L0_gnn_all.items() if k in ('Wv', 'bv', 'aw', 'ab', 'Wk', 'bk')}
    del _L0_gnn_all

    def _L1_gnn_setup():
        import jax, jax.numpy as jnp
        import numpy as np
        EPS = 1e-06
        key = jax.random.key(seed)
        k1, k2, k3 = jax.random.split(key, 3)
        B, N, F, O = (8, 2048, 256, 256)
        x = jax.random.normal(k1, (B, N, F), dtype=jnp.float32)
        adj = jax.random.uniform(k2, (B, N, N), dtype=jnp.float32)
        W = jax.random.normal(k3, (O, 2 * F), dtype=jnp.float32) * (1.0 / np.sqrt(2 * F))
        return {'x': x, 'adj': adj, 'W': W}
    _L1_gnn_all = _L1_gnn_setup()
    _L1_gnn_in = {k: v for k, v in _L1_gnn_all.items() if k in ('W',)}
    del _L1_gnn_all
    return {'x': x, 'adj': adj, 'L0_gnn_Wv': _L0_gnn_in['Wv'], 'L0_gnn_bv': _L0_gnn_in['bv'], 'L0_gnn_aw': _L0_gnn_in['aw'], 'L0_gnn_ab': _L0_gnn_in['ab'], 'L0_gnn_Wk': _L0_gnn_in['Wk'], 'L0_gnn_bk': _L0_gnn_in['bk'], 'L1_gnn_W': _L1_gnn_in['W']}

def reference(x, adj, L0_gnn_Wv, L0_gnn_bv, L0_gnn_aw, L0_gnn_ab, L0_gnn_Wk, L0_gnn_bk, L1_gnn_W):
    import jax
    import jax.numpy as jnp

    def _L0_gnn_ref(X, A, Wv, bv, aw, ab, Wk, bk):
        import jax, jax.numpy as jnp
        import numpy as np
        B, N, DIN, DOUT, K = (4, 1024, 256, 256, 3)
        d = Wv.shape[1]
        Xw = X @ Wv + bv
        sj = Xw @ aw[:d, 0]
        si = Xw @ aw[d:, 0]
        e = jax.nn.leaky_relu(sj[:, None, :] + si[:, :, None] + ab[0], negative_slope=0.2)
        alpha_matrix = A * jnp.exp(e)
        transition = alpha_matrix / (jnp.sum(alpha_matrix, axis=-1, keepdims=True) + 1e-12)
        H = jnp.zeros(X.shape[:-1] + (d,), dtype=X.dtype)
        Xk = X
        for k in range(Wk.shape[0]):
            H = H + Xk @ Wk[k] + bk[k]
            Xk = jnp.einsum('bij,bjd->bid', transition, Xk)
        return jax.nn.relu(H)

    def _L1_gnn_ref(x, adj, W):
        import jax, jax.numpy as jnp
        import numpy as np
        EPS = 1e-06
        deg = jnp.sum(adj, axis=-1, keepdims=True)
        agg = jnp.einsum('bij,bjf->bif', adj, x) / jnp.maximum(deg, EPS)
        cat = jnp.concatenate([x, agg], axis=2)
        out = jnp.einsum('bnf,of->bno', cat, W)
        return jax.nn.relu(out)
    x = _layernorm(x + _L0_gnn_ref(x, adj, L0_gnn_Wv, L0_gnn_bv, L0_gnn_aw, L0_gnn_ab, L0_gnn_Wk, L0_gnn_bk), axis=-1)
    x = _layernorm(x + _L1_gnn_ref(x, adj, L1_gnn_W), axis=-1)
    return x

_drawn_inputs = setup_inputs


def setup_inputs(seed=0):
    import zlib

    import numpy as np

    out = dict(_drawn_inputs(seed))
    spreads = {}
    factors = {'L0_gnn_Wv': 3.249, 'L0_gnn_bv': 8.0, 'L0_gnn_aw': 3.373}
    for name, (base, spread) in spreads.items():
        noise = np.random.default_rng([zlib.crc32(name.encode()), seed]).standard_normal(out[name].shape)
        drawn = base * np.exp(spread * noise) if base else spread * noise
        out[name] = jnp.asarray(drawn.astype(out[name].dtype))
    for name, factor in factors.items():
        out[name] = (out[name] * factor).astype(out[name].dtype)
    return out
```

```python
import concourse.bass as bass
from concourse import mybir
from contextlib import ExitStack


def build(nc, x_in, adj_in, wv_in, bv_in, aw_in, ab_in, wk_in, bk_in, w1_in, out):
    f32, f32r = mybir.dt.float32, mybir.dt.float32r
    ALU, ACT, AX = mybir.AluOpType, mybir.ActivationFunctionType, mybir.AxisListType

    GRAPHS, N, D = x_in.shape
    P = 128
    NB = N // P
    DB = D // P
    LN_EPS, SUM_EPS, DEG_EPS, SLOPE = 1e-5, 1e-12, 1e-6, 0.2
    COLS = 4
    SJ, SI, SI_SLOPED = 0, 1, 2
    XSLOTS = 4
    UNROLL = 4
    FIRST_LOOPED = 2
    LOOPED = (GRAPHS - 2 - FIRST_LOOPED) // UNROLL * UNROLL
    BEFORE = list(range(-2, FIRST_LOOPED))
    AFTER = list(range(FIRST_LOOPED + LOOPED, GRAPHS + 2))

    x_rows = x_in.rearrange("g (b p) d -> g p b d", p=P)
    adj_rows = adj_in.rearrange("g (b p) d -> g p b d", p=P)
    out_rows = out.rearrange("g (b p) d -> g p b d", p=P)

    def here(base, c):
        return not isinstance(base, int) or 0 <= c < GRAPHS

    def done(base, c):
        return base + (c + 1)

    def landed(base, c, slots):
        return base * (16 // slots) + 16 * (c // slots + 1)

    ctx = ExitStack()
    with ctx:
        def sb(name, shape, dt=f32):
            return ctx.enter_context(nc.sbuf_tensor(name, shape, dt))

        def sem(name):
            return ctx.enter_context(nc.semaphore(name))

        x = sb("x", [P, XSLOTS, NB, D])
        adj = sb("adj", [P, 2, NB, N])
        xt_hi, xt_lo = sb("xt_hi", [P, 4, DB, N], f32r), sb("xt_lo", [P, 4, DB, N], f32r)
        u_hi, u_lo = sb("u_hi", [P, 2, NB, D], f32r), sb("u_lo", [P, 2, NB, D], f32r)
        v_hi, v_lo = sb("v_hi", [P, NB, D], f32r), sb("v_lo", [P, NB, D], f32r)
        tt_hi, tt_lo = sb("tt_hi", [P, NB, N], f32r), sb("tt_lo", [P, NB, N], f32r)
        bt_hi, bt_lo = sb("bt_hi", [P, 2, NB, N], f32r), sb("bt_lo", [P, 2, NB, N], f32r)
        x1t_hi, x1t_lo = sb("x1t_hi", [P, DB, N], f32r), sb("x1t_lo", [P, DB, N], f32r)
        g_hi, g_lo = sb("g_hi", [P, NB, D], f32r), sb("g_lo", [P, NB, D], f32r)
        steep, gentle = sb("steep", [P, NB, N]), sb("gentle", [P, NB, N])
        trans = sb("trans", [P, NB, N])
        badj = sb("badj", [P, NB, N])
        y1 = sb("y1", [P, NB, D])
        x1 = sb("x1", [P, 2, NB, D])
        y2 = sb("y2", [P, NB, D])
        res = sb("res", [P, 2, NB, D])
        scores = sb("scores", [P, NB, COLS])
        row_sum, row_inv = sb("row_sum", [P, NB]), sb("row_inv", [P, NB])
        deg, deg_inv = sb("deg", [P, NB]), sb("deg_inv", [P, NB])
        deg_scratch = sb("deg_scratch", [P, NB, N])
        bn1, bn2 = sb("bn1", [P, NB, 6]), sb("bn2", [P, NB, 6])
        mv1, mv2 = sb("mv1", [P, NB, 2]), sb("mv2", [P, NB, 2])
        ln_var, ln_rstd, ln_shift = (sb(f"ln_{name}", [P, 2, NB]) for name in ("var", "rstd", "shift"))

        w2_hi, w2_lo = sb("w2_hi", [P, DB, D + COLS], f32r), sb("w2_lo", [P, DB, D + COLS], f32r)
        w1_hi, w1_lo = sb("w1_hi", [P, DB, D], f32r), sb("w1_lo", [P, DB, D], f32r)
        w0_hi, w0_lo = sb("w0_hi", [P, DB, D], f32r), sb("w0_lo", [P, DB, D], f32r)
        wx_hi, wx_lo = sb("wx_hi", [P, DB, D], f32r), sb("wx_lo", [P, DB, D], f32r)
        wa_hi, wa_lo = sb("wa_hi", [P, DB, D], f32r), sb("wa_lo", [P, DB, D], f32r)
        wk = sb("wk", [P, 3, DB, D])
        wv = sb("wv", [P, DB, D])
        wcat = sb("wcat", [P, D // P, 2 * D])
        aw = sb("aw", [P, 2, D])
        bv, ab, bk = sb("bv", [P, D]), sb("ab", [P, 1]), sb("bk", [P, 3, D])
        bias01, bias = sb("bias01", [P, D]), sb("bias", [P, D])
        w2s = sb("w2s", [P, DB, COLS])
        score_scratch = sb("score_scratch", [P, D])
        const_parts, score_const = sb("const_parts", [P, 3]), sb("score_const", [P, COLS])
        minus_half, minus_one, ln_eps = sb("minus_half", [P, NB]), sb("minus_one", [P, NB]), sb("ln_eps", [P, NB])
        ident = sb("ident", [P, P])

        def bank(name, shape):
            return ctx.enter_context(nc.psum_tensor(name, shape, f32))

        u_ps = bank("u_ps", [P, 2, 512])
        v_ps = bank("v_ps", [P, NB, D])
        h_ps = bank("h_ps", [P, NB, D])
        g_ps = bank("g_ps", [P, NB, D])
        o_ps = bank("o_ps", [P, NB, D])
        ta_ps = bank("ta_ps", [P, 2, 256])
        tb_ps = bank("tb_ps", [P, 2, 256])
        sj_ps = u_ps[:, :, 384:512]

        s_x = [sem(f"s_x{i}") for i in range(XSLOTS)]
        s_adj = [sem(f"s_adj{i}") for i in range(2)]
        s_res = [sem(f"s_res{i}") for i in range(2)]
        s_wk, s_wcat, s_wv = sem("s_wk"), sem("s_wcat"), sem("s_wv")
        s_ident0, s_ident, s_half = sem("s_ident0"), sem("s_ident"), sem("s_half")
        s_wt, s_whi, s_wlo = sem("s_wt"), sem("s_whi"), sem("s_wlo")
        s_cols, s_parts, s_const = sem("s_cols"), sem("s_parts"), sem("s_const")
        s_bias01, s_bias = sem("s_bias01"), sem("s_bias")
        p_xt, p_u, p_sj, p_tt, p_bt = sem("p_xt"), sem("p_u"), sem("p_sj"), sem("p_tt"), sem("p_bt")
        p_v, p_h, p_x1t, p_g, p_o = sem("p_v"), sem("p_h"), sem("p_x1t"), sem("p_g"), sem("p_o")
        a_xt, a_u, a_tt, a_bt = sem("a_xt"), sem("a_u"), sem("a_tt"), sem("a_bt")
        a_v, a_x1t, a_g, a_exp, a_deg = sem("a_v"), sem("a_x1t"), sem("a_g"), sem("a_exp"), sem("a_deg")
        v_xt, v_u, v_tt, v_bt = sem("v_xt"), sem("v_u"), sem("v_tt"), sem("v_bt")
        v_v, v_x1t, v_g = sem("v_v"), sem("v_x1t"), sem("v_g")
        v_degc, v_deg = sem("v_degc"), sem("v_deg")
        v_alpha, v_sum, v_inv, v_exp = sem("v_alpha"), sem("v_sum"), sem("v_inv"), sem("v_exp")
        v_hb, v_y1, v_mv1 = sem("v_hb"), sem("v_y1"), sem("v_mv1")
        v_y2, v_mv2 = sem("v_y2"), sem("v_mv2")
        g_t, g_badj, g_x1, g_res = sem("g_t"), sem("g_badj"), sem("g_x1"), sem("g_res")

        block = ctx.enter_context(nc.Block())

        @block.sync
        def _(sp):
            def load_x(base, c):
                if not here(base, c):
                    return
                if here(base, c - XSLOTS):
                    sp.wait_ge(v_y1, done(base, c - XSLOTS))
                sp.dma_start(x[:, c % XSLOTS], x_rows[base + c]).then_inc(s_x[c % XSLOTS], 16)

            def load_adj(base, c):
                if not here(base, c):
                    return
                if here(base, c - 2):
                    sp.wait_ge(v_alpha, done(base, c - 2))
                    sp.wait_ge(g_badj, done(base, c - 2))
                sp.dma_start(adj[:, c % 2], adj_rows[base + c]).then_inc(s_adj[c % 2], 16)

            def store(base, c):
                if here(base, c):
                    sp.wait_ge(g_res, done(base, c))
                    sp.dma_start(out_rows[base + c], res[:, c % 2]).then_inc(s_res[c % 2], 16)

            def iteration(base, k):
                load_x(base, k + 2)
                load_adj(base, k + 2)
                store(base, k - 2)

            load_x(0, 0)
            sp.dma_start(wk[:], wk_in.rearrange("k (b p) d -> p k b d", p=P)).then_inc(s_wk, 16)
            sp.dma_start(wv[:], wv_in.rearrange("(b p) d -> p b d", p=P)).then_inc(s_wv, 16)
            sp.dma_start(aw[:], aw_in.rearrange("(h d) one -> one h d", d=D).broadcast_to([P, 2, D])).then_inc(s_wv, 16)
            sp.dma_start(bv[:], bv_in.rearrange("(one d) -> one d", one=1).broadcast_to([P, D])).then_inc(s_wv, 16)
            sp.dma_start(ab[:], ab_in.rearrange("(one d) -> one d", one=1).broadcast_to([P, 1])).then_inc(s_wv, 16)
            sp.dma_start(bk[:], bk_in.rearrange("(one k) d -> one k d", one=1).broadcast_to([P, 3, D])).then_inc(s_wv, 16)
            load_adj(0, 0)
            sp.dma_start(wcat[:], w1_in.rearrange("(b p) f -> p b f", p=P)).then_inc(s_wcat, 16)
            load_x(0, 1)
            load_adj(0, 1)
            for k in BEFORE[2:]:
                iteration(0, k)
            with sp.Fori(0, LOOPED // UNROLL) as group:
                for k in range(FIRST_LOOPED, FIRST_LOOPED + UNROLL):
                    iteration(group * UNROLL, k)
            for k in AFTER:
                iteration(0, k)
            for slot in range(2):
                sp.wait_ge(s_res[slot], landed(0, GRAPHS - 2 + slot, 2))

        @block.gpsimd
        def _(gp):
            nc.gpsimd.memset(ident[:], 0.0).then_inc(s_ident0, 1)
            nc.gpsimd.memset(minus_half[:], -0.5).then_inc(s_half, 1)
            nc.gpsimd.memset(minus_one[:], -1.0).then_inc(s_half, 1)
            nc.gpsimd.memset(ln_eps[:], LN_EPS).then_inc(s_half, 1)
            gp.wait_ge(s_ident0, 1)
            nc.gpsimd.affine_select(out=ident[:], in_=ident[:], compare_op=ALU.not_equal, fill=1.0, base=0,
                                    pattern=[[-1, P]], channel_multiplier=1).then_inc(s_ident, 1)
            gp.wait_ge(s_half, 3)

            def normalise(layer, mv, src, dst, finished):
                nc.gpsimd.tensor_tensor(ln_var[:, layer], mv[:, :, 1], ln_eps[:], ALU.add)
                nc.gpsimd.tensor_tensor(ln_shift[:, layer], mv[:, :, 0], minus_one[:], ALU.mult)
                gp.drain()
                nc.gpsimd.tensor_tensor(ln_rstd[:, layer], ln_var[:, layer], minus_half[:], ALU.pow)
                gp.drain()
                nc.gpsimd.tensor_tensor(ln_shift[:, layer], ln_shift[:, layer], ln_rstd[:, layer], ALU.mult)
                gp.drain()
                for b in range(NB):
                    last = nc.gpsimd.tensor_scalar(dst[:, b], src[:, b], ln_rstd[:, layer, b:b + 1], ln_shift[:, layer, b:b + 1],
                                                   ALU.mult, ALU.add)
                last.then_inc(finished, 1)

            def iteration(base, k):
                if here(base, k - 2):
                    gp.wait_ge(v_mv2, done(base, k - 2))
                    if here(base, k - 4):
                        gp.wait_ge(s_res[k % 2], landed(base, k - 4, 2))
                    normalise(1, mv2, y2[:], res[:, k % 2], g_res)
                if here(base, k + 1):
                    gp.wait_ge(v_deg, done(base, k + 1))
                    if here(base, k):
                        gp.wait_ge(p_bt, done(base, k))
                    nc.gpsimd.tensor_tensor(badj[:], adj[:, (k + 1) % 2],
                                            deg_inv[:, :, None].broadcast_to([P, NB, N]), ALU.mult).then_inc(g_badj, 1)
                    gp.wait_ge(v_inv, done(base, k + 1))
                    nc.gpsimd.tensor_tensor(trans[:], trans[:], row_inv[:, :, None].broadcast_to([P, NB, N]),
                                            ALU.mult).then_inc(g_t, 1)
                if here(base, k):
                    gp.wait_ge(v_mv1, done(base, k))
                    normalise(0, mv1, y1[:], x1[:, k % 2], g_x1)

            for k in BEFORE:
                iteration(0, k)
            with gp.Fori(0, LOOPED // UNROLL) as group:
                for k in range(FIRST_LOOPED, FIRST_LOOPED + UNROLL):
                    iteration(group * UNROLL, k)
            for k in AFTER:
                iteration(0, k)

        @block.scalar
        def _(act):
            def high(dst, src, finished):
                nc.scalar.activation(dst, src, ACT.Copy).then_inc(finished, 1)

            act.wait_ge(s_wk, 16)
            high(w2_hi[:, :, 0:D], wk[:, 2], s_whi)
            act.wait_ge(s_cols, 1)
            high(w2_hi[:, :, D:D + COLS], w2s[:], s_whi)
            high(w1_hi[:], wk[:, 1], s_whi)
            high(w0_hi[:], wk[:, 0], s_whi)

            def degrees(base, c):
                if here(base, c):
                    act.wait_ge(s_adj[c % 2], landed(base, c, 2))
                    for b in range(NB):
                        last = nc.scalar.activation(deg_scratch[:, b], adj[:, c % 2, b], ACT.Copy,
                                                    accum_out=deg[:, b:b + 1])
                    last.then_inc(a_deg, 1)

            def iteration(base, k):
                if here(base, k):
                    act.wait_ge(p_bt, done(base, k))
                    high(bt_hi[:, k % 2], ta_ps[:], a_bt)
                    act.wait_ge(p_tt, done(base, k))
                    high(tt_hi[:], tb_ps[:], a_tt)
                if here(base, k + 1):
                    act.wait_ge(p_u, done(base, k + 1))
                    high(u_hi[:, (k + 1) % 2], u_ps[:, :, 0:D], a_u)
                if here(base, k - 1):
                    act.wait_ge(p_x1t, done(base, k - 1))
                    high(x1t_hi[:], ta_ps[:], a_x1t)
                if here(base, k):
                    act.wait_ge(p_v, done(base, k))
                    high(v_hi[:], v_ps[:], a_v)
                if here(base, k + 2):
                    act.wait_ge(p_xt, done(base, k + 2))
                    high(xt_hi[:, (k + 2) % 4], tb_ps[:], a_xt)
                if here(base, k + 1):
                    act.wait_ge(p_sj, done(base, k + 1))
                    for b in range(NB):
                        nc.scalar.activation(steep[:, b].rearrange("p (j q) -> p j q", q=P), sj_ps, ACT.Exp,
                                             bias=scores[:, b, SI:SI + 1])
                        last = nc.scalar.activation(gentle[:, b].rearrange("p (j q) -> p j q", q=P), sj_ps, ACT.Exp,
                                                    bias=scores[:, b, SI_SLOPED:SI_SLOPED + 1], scale=SLOPE)
                    last.then_inc(a_exp, 1)
                if here(base, k - 1):
                    act.wait_ge(p_g, done(base, k - 1))
                    high(g_hi[:], g_ps[:], a_g)
                degrees(base, k + 2)

            for k in BEFORE:
                if k == -2:
                    degrees(0, 0)
                    act.wait_ge(s_wt, 1)
                    high(wx_hi[:], v_ps[:], s_whi)
                    high(wa_hi[:], h_ps[:], s_whi)
                    act.wait_ge(p_xt, done(0, 0))
                    high(xt_hi[:, 0], tb_ps[:], a_xt)
                elif k == -1:
                    act.wait_ge(p_u, done(0, 0))
                    high(u_hi[:, 0], u_ps[:, :, 0:D], a_u)
                    act.wait_ge(p_xt, done(0, 1))
                    high(xt_hi[:, 1], tb_ps[:], a_xt)
                    act.wait_ge(p_sj, done(0, 0))
                    for b in range(NB):
                        nc.scalar.activation(steep[:, b].rearrange("p (j q) -> p j q", q=P), sj_ps, ACT.Exp,
                                             bias=scores[:, b, SI:SI + 1])
                        last = nc.scalar.activation(gentle[:, b].rearrange("p (j q) -> p j q", q=P), sj_ps, ACT.Exp,
                                                    bias=scores[:, b, SI_SLOPED:SI_SLOPED + 1], scale=SLOPE)
                    last.then_inc(a_exp, 1)
                    act.wait_ge(v_deg, done(0, 0))
                    degrees(0, 1)
                else:
                    iteration(0, k)
            with act.Fori(0, LOOPED // UNROLL) as group:
                for k in range(FIRST_LOOPED, FIRST_LOOPED + UNROLL):
                    iteration(group * UNROLL, k)
            for k in AFTER:
                iteration(0, k)

        @block.vector
        def _(dve):
            def low(dst, src, hi, finished):
                nc.vector.tensor_tensor(dst, src, hi.bitcast(f32), ALU.subtract).then_inc(finished, 1)

            dve.wait_ge(s_wv, 16 * 5)
            nc.vector.memset(w2s[:], 0.0).then_inc(s_parts, 1)
            nc.vector.memset(score_const[:], 0.0).then_inc(s_parts, 1)
            dve.wait_ge(s_parts, 2)
            for b in range(DB):
                for col in (SJ, SI):
                    nc.vector.scalar_tensor_tensor(score_scratch[:], wv[:, b], 1.0, aw[:, col], ALU.mult, ALU.mult,
                                                   accum_out=w2s[:, b, col:col + 1]).then_inc(s_parts, 1)
                    dve.wait_ge(s_parts, 3 + 2 * b + col)
            for col in (SJ, SI):
                nc.vector.scalar_tensor_tensor(score_scratch[:], bv[:], 1.0, aw[:, col], ALU.mult, ALU.mult,
                                               accum_out=const_parts[:, col:col + 1]).then_inc(s_parts, 1)
                dve.wait_ge(s_parts, 7 + col)
            nc.vector.tensor_scalar(w2s[:, :, SI_SLOPED], w2s[:, :, SI], SLOPE, None, ALU.mult).then_inc(s_cols, 1)
            nc.vector.scalar_tensor_tensor(score_const[:, SI:SI + 1], const_parts[:, 0:1], ab[:], const_parts[:, 1:2],
                                           ALU.add, ALU.add).then_inc(s_const, 1)
            nc.vector.tensor_tensor(bias01[:], bk[:, 0], bk[:, 1], ALU.add).then_inc(s_bias01, 1)
            dve.wait_ge(s_const, 1)
            nc.vector.tensor_scalar(score_const[:, SI_SLOPED:SI_SLOPED + 1], score_const[:, SI:SI + 1], SLOPE, None,
                                    ALU.mult).then_inc(s_const, 1)
            dve.wait_ge(s_bias01, 1)
            nc.vector.tensor_tensor(bias[:], bias01[:], bk[:, 2], ALU.add).then_inc(s_bias, 1)
            dve.wait_ge(s_whi, 2)
            low(w2_lo[:, :, 0:D], wk[:, 2], w2_hi[:, :, 0:D], s_wlo)
            dve.wait_ge(s_cols, 1)
            low(w2_lo[:, :, D:D + COLS], w2s[:], w2_hi[:, :, D:D + COLS], s_wlo)
            dve.wait_ge(s_whi, 4)
            low(w1_lo[:], wk[:, 1], w1_hi[:], s_wlo)
            low(w0_lo[:], wk[:, 0], w0_hi[:], s_wlo)
            dve.wait_ge(s_const, 2)
            dve.wait_ge(s_bias, 1)

            def degrees(base, c):
                if here(base, c):
                    if here(base, c - 1):
                        dve.wait_ge(g_badj, done(base, c - 1))
                    dve.wait_ge(a_deg, done(base, c))
                    nc.vector.tensor_scalar(deg_inv[:], deg[:], DEG_EPS, None, ALU.max).then_inc(v_degc, 1)
                    dve.wait_ge(v_degc, done(base, c))
                    nc.vector.reciprocal(deg_inv[:], deg_inv[:]).then_inc(v_deg, 1)

            def split_u(base, c):
                if here(base, c):
                    dve.wait_ge(a_u, done(base, c))
                    nc.vector.tensor_tensor(scores[:], u_ps[:, :, D:D + COLS],
                                            score_const[:, None, :].broadcast_to([P, NB, COLS]), ALU.add)
                    low(u_lo[:, c % 2], u_ps[:, :, 0:D], u_hi[:, c % 2], v_u)

            def split_xt(base, c):
                if here(base, c):
                    dve.wait_ge(a_xt, done(base, c))
                    low(xt_lo[:, c % 4], tb_ps[:], xt_hi[:, c % 4], v_xt)

            def edge_weights(base, c):
                if here(base, c):
                    dve.wait_ge(a_exp, done(base, c))
                    nc.vector.tensor_tensor(steep[:], steep[:], gentle[:], ALU.max).then_inc(v_exp, 1)
                    dve.wait_ge(v_exp, done(base, c))
                    for b in range(NB):
                        last = nc.vector.scalar_tensor_tensor(trans[:, b], adj[:, c % 2, b], 1.0, steep[:, b],
                                                              ALU.mult, ALU.mult, accum_out=row_sum[:, b:b + 1])
                    last.then_inc(v_alpha, 1)
                    dve.wait_ge(v_alpha, done(base, c))
                    nc.vector.tensor_scalar(row_inv[:], row_sum[:], SUM_EPS, None, ALU.add).then_inc(v_sum, 1)
                    dve.wait_ge(v_sum, done(base, c))
                    nc.vector.reciprocal(row_inv[:], row_inv[:]).then_inc(v_inv, 1)

            def statistics(base, c, y, written, bn, mv, finished):
                dve.wait_ge(written, done(base, c))
                for b in range(NB):
                    nc.vector.bn_stats(bn[:, b], y[:, b])
                dve.drain()
                for b in range(NB):
                    last = nc.vector.bn_aggr(mv[:, b], bn[:, b])
                last.then_inc(finished, 1)

            def iteration(base, k):
                degrees(base, k + 1)
                if here(base, k):
                    dve.wait_ge(a_bt, done(base, k))
                    low(bt_lo[:, k % 2], ta_ps[:], bt_hi[:, k % 2], v_bt)
                    dve.wait_ge(a_tt, done(base, k))
                    low(tt_lo[:], tb_ps[:], tt_hi[:], v_tt)
                split_u(base, k + 1)
                if here(base, k - 1):
                    dve.wait_ge(a_x1t, done(base, k - 1))
                    low(x1t_lo[:], ta_ps[:], x1t_hi[:], v_x1t)
                if here(base, k):
                    dve.wait_ge(a_v, done(base, k))
                    low(v_lo[:], v_ps[:], v_hi[:], v_v)
                split_xt(base, k + 2)
                if here(base, k - 1):
                    dve.wait_ge(a_g, done(base, k - 1))
                    low(g_lo[:], g_ps[:], g_hi[:], v_g)
                edge_weights(base, k + 1)
                if here(base, k):
                    dve.wait_ge(p_h, done(base, k))
                    nc.vector.tensor_tensor(y1[:], h_ps[:], bias[:, None, :].broadcast_to([P, NB, D]),
                                            ALU.add).then_inc(v_hb, 1)
                    dve.wait_ge(v_hb, done(base, k))
                    nc.vector.scalar_tensor_tensor(y1[:], y1[:], 0.0, x[:, k % XSLOTS], ALU.max,
                                                   ALU.add).then_inc(v_y1, 1)
                    statistics(base, k, y1[:], v_y1, bn1[:], mv1[:], v_mv1)
                if here(base, k - 1):
                    dve.wait_ge(p_o, done(base, k - 1))
                    if here(base, k - 2):
                        dve.wait_ge(g_res, done(base, k - 2))
                    nc.vector.scalar_tensor_tensor(y2[:], o_ps[:], 0.0, x1[:, (k - 1) % 2], ALU.max,
                                                   ALU.add).then_inc(v_y2, 1)
                    statistics(base, k - 1, y2[:], v_y2, bn2[:], mv2[:], v_mv2)

            for k in BEFORE:
                if k == -2:
                    dve.wait_ge(s_whi, 6)
                    low(wx_lo[:], v_ps[:], wx_hi[:], s_wlo)
                    low(wa_lo[:], h_ps[:], wa_hi[:], s_wlo)
                    split_xt(0, 0)
                elif k == -1:
                    degrees(0, 0)
                    split_u(0, 0)
                    split_xt(0, 1)
                    edge_weights(0, 0)
                else:
                    iteration(0, k)
            with dve.Fori(0, LOOPED // UNROLL) as group:
                for k in range(FIRST_LOOPED, FIRST_LOOPED + UNROLL):
                    iteration(group * UNROLL, k)
            for k in AFTER:
                iteration(0, k)

        @block.tensor
        def _(pe):
            def product(dst, left, right, b, first):
                left_hi, left_lo = left
                right_hi, right_lo = right
                rows = slice(b * P, (b + 1) * P)
                for lh, rh in ((left_hi, right_lo), (left_lo, right_hi), (left_hi, right_hi)):
                    for kb in range(2):
                        last = nc.tensor.matmul(dst, lh[:, kb, rows], rh[:, kb], start=first, stop=True,
                                                skip_group_check=True)
                        first = False
                return last

            def transposed(dst, src):
                for c in range(2):
                    for r in range(2):
                        last = nc.tensor.transpose(dst[:, c, r * P:(r + 1) * P], src[:, r, c * P:(c + 1) * P],
                                                   ident[:])
                return last

            def transpose_x(base, c):
                if here(base, c):
                    pe.wait_ge(s_x[c % XSLOTS], landed(base, c, XSLOTS))
                    transposed(tb_ps, x[:, c % XSLOTS]).then_inc(p_xt, 1)

            def iteration(base, k):
                xt = [(xt_hi[:, (k + i) % 4], xt_lo[:, (k + i) % 4]) for i in range(2)]
                u = (u_hi[:, k % 2], u_lo[:, k % 2])
                if here(base, k):
                    for b in range(NB):
                        product(v_ps[:, b], xt[0], (w1_hi, w1_lo), b, b == 0)
                if here(base, k + 1):
                    pe.wait_ge(v_xt, done(base, k + 1))
                    for b in range(NB):
                        last = product(u_ps[:, b, 0:D + COLS], xt[1], (w2_hi, w2_lo), b, True)
                    last.then_inc(p_u, 1)
                if here(base, k - 1):
                    pe.wait_ge(g_x1, done(base, k - 1))
                    if here(base, k):
                        pe.wait_ge(v_bt, done(base, k))
                    transposed(ta_ps, x1[:, (k - 1) % 2]).then_inc(p_x1t, 1)
                if here(base, k):
                    pe.wait_ge(v_tt, done(base, k))
                    for b in range(NB):
                        last = product(v_ps[:, b], (tt_hi, tt_lo), u, b, False)
                    last.then_inc(p_v, 1)
                transpose_x(base, k + 2)
                if here(base, k + 1):
                    pe.wait_ge(v_u, done(base, k + 1))
                    for b in range(NB):
                        last = nc.tensor.transpose(sj_ps[:, b], scores[:, b, SJ:SJ + 1].broadcast_to([P, P]), ident[:])
                    last.then_inc(p_sj, 1)
                if here(base, k - 1):
                    pe.wait_ge(v_x1t, done(base, k - 1))
                    for b in range(NB):
                        last = product(g_ps[:, b], (x1t_hi, x1t_lo), (wa_hi, wa_lo), b, b == 0)
                    last.then_inc(p_g, 1)
                if here(base, k):
                    for b in range(NB):
                        product(h_ps[:, b], xt[0], (w0_hi, w0_lo), b, b == 0)
                    pe.wait_ge(v_v, done(base, k))
                    for b in range(NB):
                        last = product(h_ps[:, b], (tt_hi, tt_lo), (v_hi, v_lo), b, False)
                    last.then_inc(p_h, 1)
                if here(base, k - 1):
                    if here(base, k - 2):
                        pe.wait_ge(v_y2, done(base, k - 2))
                    for b in range(NB):
                        product(o_ps[:, b], (x1t_hi, x1t_lo), (wx_hi, wx_lo), b, b == 0)
                    pe.wait_ge(v_g, done(base, k - 1))
                    for b in range(NB):
                        last = product(o_ps[:, b], (bt_hi[:, (k - 1) % 2], bt_lo[:, (k - 1) % 2]), (g_hi, g_lo), b, False)
                    last.then_inc(p_o, 1)
                if here(base, k + 1):
                    pe.wait_ge(g_badj, done(base, k + 1))
                    transposed(ta_ps, badj).then_inc(p_bt, 1)
                    pe.wait_ge(g_t, done(base, k + 1))
                    if here(base, k + 2):
                        pe.wait_ge(v_xt, done(base, k + 2))
                    transposed(tb_ps, trans).then_inc(p_tt, 1)

            pe.wait_ge(s_ident, 1)
            transpose_x(0, 0)
            pe.wait_ge(s_wcat, 16)
            transposed(v_ps, wcat[:, :, 0:D])
            transposed(h_ps, wcat[:, :, D:2 * D]).then_inc(s_wt, 1)
            pe.wait_ge(s_wlo, 6)
            for k in BEFORE[1:]:
                iteration(0, k)
            with pe.Fori(0, LOOPED // UNROLL) as group:
                for k in range(FIRST_LOOPED, FIRST_LOOPED + UNROLL):
                    iteration(group * UNROLL, k)
            for k in AFTER:
                iteration(0, k)


_INS = ["x", "adj", "L0_gnn_Wv", "L0_gnn_bv", "L0_gnn_aw", "L0_gnn_ab", "L0_gnn_Wk", "L0_gnn_bk", "L1_gnn_W"]


def kernel(**inputs):
    import numpy as np
    import concourse.bacc as bacc
    from concourse.bass_utils import run_bass_kernel_spmd

    nc = bacc.Bacc("TRN2", target_bir_lowering=False, num_devices=1)
    arrays, args = {}, []
    for name in _INS:
        a = np.ascontiguousarray(inputs[name])
        arrays[f"in_{name}"] = a
        args.append(nc.dram_tensor(f"in_{name}", a.shape, mybir.dt.from_np(a.dtype), kind="ExternalInput").ap())
    out = nc.dram_tensor("result", arrays["in_x"].shape, mybir.dt.float32, kind="ExternalOutput").ap()
    build(nc, *args, out)
    r = run_bass_kernel_spmd(nc, [arrays], core_ids=[0])
    return r.results[0]["result"]
```

```python
import concourse.bass as bass
from concourse import mybir
from contextlib import ExitStack


def build(nc, x_in, adj_in, wv_in, bv_in, aw_in, ab_in, wk_in, bk_in, w1_in, out):
    f32, f32r = mybir.dt.float32, mybir.dt.float32r
    ALU, ACT, AX = mybir.AluOpType, mybir.ActivationFunctionType, mybir.AxisListType

    GRAPHS, N, D = x_in.shape
    P = 128
    NB = N // P
    DB = D // P
    LN_EPS, SUM_EPS, DEG_EPS, SLOPE = 1e-5, 1e-12, 1e-6, 0.2
    COLS = 4
    SJ, SI, SI_SLOPED = 0, 1, 2
    TILE = 32
    UNROLL = 4
    FIRST_LOOPED = 2
    LOOPED = (GRAPHS - 2 - FIRST_LOOPED) // UNROLL * UNROLL
    BEFORE = list(range(-2, FIRST_LOOPED))
    AFTER = list(range(FIRST_LOOPED + LOOPED, GRAPHS + 2))

    x_rows = x_in.rearrange("g (b p) d -> g p b d", p=P)
    x_tiles = x_in.rearrange("g (q a) (d c b) -> g c a d q b", a=TILE, b=TILE, c=P // TILE)
    adj_rows = adj_in.rearrange("g (b p) d -> g p b d", p=P)
    out_rows = out.rearrange("g (b p) d -> g p b d", p=P)

    def here(base, c):
        return not isinstance(base, int) or 0 <= c < GRAPHS

    def done(base, c):
        return base + (c + 1)

    def done_block(base, c, b):
        return base * NB + (c * NB + b + 1)

    def landed(base, c, transfers=1):
        return base * (8 * transfers) + 16 * transfers * (c // 2 + 1)

    ctx = ExitStack()
    with ctx:
        def sb(name, shape, dt=f32):
            return ctx.enter_context(nc.sbuf_tensor(name, shape, dt))

        def sem(name):
            return ctx.enter_context(nc.semaphore(name))

        x = sb("x", [P, 2, NB, D])
        xs = sb("xs", [P, 2, DB, N // TILE, TILE])
        xt = sb("xt", [P, DB, N])
        adj = sb("adj", [P, 2, NB, N])
        xt_hi, xt_lo = sb("xt_hi", [P, 2, DB, N], f32r), sb("xt_lo", [P, 2, DB, N], f32r)
        u_hi, u_lo = sb("u_hi", [P, 2, NB, D], f32r), sb("u_lo", [P, 2, NB, D], f32r)
        v_hi, v_lo = sb("v_hi", [P, NB, D], f32r), sb("v_lo", [P, NB, D], f32r)
        tt_hi, tt_lo = sb("tt_hi", [P, NB, N], f32r), sb("tt_lo", [P, NB, N], f32r)
        bt_hi, bt_lo = sb("bt_hi", [P, 2, NB, N], f32r), sb("bt_lo", [P, 2, NB, N], f32r)
        x1t_hi, x1t_lo = sb("x1t_hi", [P, DB, N], f32r), sb("x1t_lo", [P, DB, N], f32r)
        g_hi, g_lo = sb("g_hi", [P, NB, D], f32r), sb("g_lo", [P, NB, D], f32r)
        steep, gentle = sb("steep", [P, NB, N]), sb("gentle", [P, NB, N])
        trans = sb("trans", [P, NB, N])
        badj = sb("badj", [P, NB, N])
        y1 = sb("y1", [P, NB, D])
        x1 = sb("x1", [P, 2, NB, D])
        y2 = sb("y2", [P, NB, D])
        res = sb("res", [P, 2, NB, D])
        scores = sb("scores", [P, NB, COLS])
        row_sum, row_inv = sb("row_sum", [P, NB]), sb("row_inv", [P, NB])
        deg, deg_inv = sb("deg", [P, NB]), sb("deg_inv", [P, NB])
        deg_scratch = sb("deg_scratch", [P, NB, N])
        bn1, bn2 = sb("bn1", [P, NB, 6]), sb("bn2", [P, NB, 6])
        mv1, mv2 = sb("mv1", [P, NB, 2]), sb("mv2", [P, NB, 2])
        ln_var, ln_rstd, ln_shift = (sb(f"ln_{name}", [P, 2, NB]) for name in ("var", "rstd", "shift"))

        w2_hi, w2_lo = sb("w2_hi", [P, DB, D + COLS], f32r), sb("w2_lo", [P, DB, D + COLS], f32r)
        w10_hi, w10_lo = sb("w10_hi", [P, DB, 2 * D], f32r), sb("w10_lo", [P, DB, 2 * D], f32r)
        wax_hi, wax_lo = sb("wax_hi", [P, DB, 2 * D], f32r), sb("wax_lo", [P, DB, 2 * D], f32r)
        wk = sb("wk", [P, 3, DB, D])
        wv = sb("wv", [P, DB, D])
        wcat = sb("wcat", [P, D // P, 2 * D])
        aw = sb("aw", [P, 2, D])
        bv, ab, bk = sb("bv", [P, D]), sb("ab", [P, 1]), sb("bk", [P, 3, D])
        bias01, bias = sb("bias01", [P, D]), sb("bias", [P, D])
        w2s = sb("w2s", [P, DB, COLS])
        score_scratch = sb("score_scratch", [P, 6, D])
        const_parts, score_const = sb("const_parts", [P, 3]), sb("score_const", [P, COLS])
        minus_half, minus_one, ln_eps = sb("minus_half", [P, NB]), sb("minus_one", [P, NB]), sb("ln_eps", [P, NB])
        ident = sb("ident", [P, P])

        def bank(name, shape):
            return ctx.enter_context(nc.psum_tensor(name, shape, f32))

        u_ps = bank("u_ps", [P, 2, 512])
        vh_ps = bank("vh_ps", [P, 2, 512])
        go_ps = bank("go_ps", [P, 2, 512])
        ta_ps = bank("ta_ps", [P, 2, 256])
        tb_ps = bank("tb_ps", [P, 2, 256])
        sj_ps = u_ps[:, :, 384:512]
        v_ps, h_ps = vh_ps[:, :, 0:D], vh_ps[:, :, D:2 * D]
        g_ps, o_ps = go_ps[:, :, 0:D], go_ps[:, :, D:2 * D]

        s_x = [sem(f"s_x{i}") for i in range(2)]
        s_xs = [sem(f"s_xs{i}") for i in range(2)]
        s_adj = [sem(f"s_adj{i}") for i in range(2)]
        s_res = [sem(f"s_res{i}") for i in range(2)]
        s_wk = [sem(f"s_wk{i}") for i in range(3)]
        s_wcat, s_wv, s_const_in, s_bk = sem("s_wcat"), sem("s_wv"), sem("s_const_in"), sem("s_bk")
        s_ident0, s_ident, s_half = sem("s_ident0"), sem("s_ident"), sem("s_half")
        s_wt = sem("s_wt")
        s_whi, s_wlo = sem("s_whi"), sem("s_wlo")
        W2, W2_COLS, W1, W0, WX, WA = range(1, 7)
        s_cols, s_parts, s_const = sem("s_cols"), sem("s_parts"), sem("s_const")
        s_bias01, s_bias = sem("s_bias01"), sem("s_bias")
        p_u, p_sj, p_tt, p_bt = sem("p_u"), sem("p_sj"), sem("p_tt"), sem("p_bt")
        p_v, p_h, p_x1t, p_g, p_o = sem("p_v"), sem("p_h"), sem("p_x1t"), sem("p_g"), sem("p_o")
        a_xt, a_u, a_tt, a_bt = sem("a_xt"), sem("a_u"), sem("a_tt"), sem("a_bt")
        a_v, a_x1t, a_g, a_exp, a_deg = sem("a_v"), sem("a_x1t"), sem("a_g"), sem("a_exp"), sem("a_deg")
        v_xt = sem("v_xt")
        v_u, v_tt, v_bt = sem("v_u"), sem("v_tt"), sem("v_bt")
        v_v, v_x1t, v_g = sem("v_v"), sem("v_x1t"), sem("v_g")
        v_degc, v_deg = sem("v_degc"), sem("v_deg")
        v_alpha, v_sum, v_inv, v_exp = sem("v_alpha"), sem("v_sum"), sem("v_inv"), sem("v_exp")
        v_hb, v_y1, v_mv1 = sem("v_hb"), sem("v_y1"), sem("v_mv1")
        v_y2, v_mv2 = sem("v_y2"), sem("v_mv2")
        g_xt = sem("g_xt")
        g_t, g_badj, g_x1, g_res = sem("g_t"), sem("g_badj"), sem("g_x1"), sem("g_res")

        block = ctx.enter_context(nc.Block())

        @block.sync
        def _(sp):
            def load_x(base, c):
                if here(base, c):
                    if here(base, c - 2):
                        sp.wait_ge(v_y1, done(base, c - 2))
                    sp.dma_start(x[:, c % 2], x_rows[base + c]).then_inc(s_x[c % 2], 16)

            def load_tiles(base, c):
                if here(base, c):
                    if here(base, c - 2):
                        sp.wait_ge(v_xt, done(base, c - 2))
                    for t in range(P // TILE):
                        sp.dma_start(xs[t * TILE:(t + 1) * TILE, c % 2], x_tiles[base + c, t]).then_inc(s_xs[c % 2], 16)

            def load_adj(base, c):
                if not here(base, c):
                    return
                if here(base, c - 2):
                    sp.wait_ge(v_alpha, done(base, c - 2))
                    sp.wait_ge(g_badj, done(base, c - 2))
                sp.dma_start(adj[:, c % 2], adj_rows[base + c]).then_inc(s_adj[c % 2], 16)

            def store(base, c):
                if here(base, c):
                    sp.wait_ge(g_res, done(base, c))
                    sp.dma_start(out_rows[base + c], res[:, c % 2]).then_inc(s_res[c % 2], 16)

            def iteration(base, k):
                load_tiles(base, k + 2)
                load_adj(base, k + 2)
                load_x(base, k + 1)
                store(base, k - 2)

            def load_wk(i):
                sp.dma_start(wk[:, i], wk_in[i].rearrange("(b p) d -> p b d", p=P)).then_inc(s_wk[i], 16)

            load_tiles(0, 0)
            load_wk(2)
            load_adj(0, 0)
            load_tiles(0, 1)
            load_wk(1)
            sp.dma_start(wcat[:], w1_in.rearrange("(b p) f -> p b f", p=P)).then_inc(s_wcat, 16)
            load_wk(0)
            load_adj(0, 1)
            load_x(0, 0)
            for k in BEFORE[2:]:
                iteration(0, k)
            with sp.Fori(0, LOOPED // UNROLL) as group:
                for k in range(FIRST_LOOPED, FIRST_LOOPED + UNROLL):
                    iteration(group * UNROLL, k)
            for k in AFTER:
                iteration(0, k)
            for slot in range(2):
                sp.wait_ge(s_res[slot], landed(0, GRAPHS - 2 + slot))

        @block.gpsimd
        def _(gp):
            nc.gpsimd.memset(ident[:], 0.0).then_inc(s_ident0, 1)
            nc.gpsimd.memset(minus_half[:], -0.5).then_inc(s_half, 1)
            nc.gpsimd.memset(minus_one[:], -1.0).then_inc(s_half, 1)
            nc.gpsimd.memset(ln_eps[:], LN_EPS).then_inc(s_half, 1)
            gp.wait_ge(s_ident0, 1)
            nc.gpsimd.affine_select(out=ident[:], in_=ident[:], compare_op=ALU.not_equal, fill=1.0, base=0,
                                    pattern=[[-1, P]], channel_multiplier=1).then_inc(s_ident, 1)
            gp.wait_ge(s_half, 3)

            def normalise(layer, mv, src, dst, finished):
                nc.gpsimd.tensor_tensor(ln_var[:, layer], mv[:, :, 1], ln_eps[:], ALU.add)
                nc.gpsimd.tensor_tensor(ln_shift[:, layer], mv[:, :, 0], minus_one[:], ALU.mult)
                gp.drain()
                nc.gpsimd.tensor_tensor(ln_rstd[:, layer], ln_var[:, layer], minus_half[:], ALU.pow)
                gp.drain()
                nc.gpsimd.tensor_tensor(ln_shift[:, layer], ln_shift[:, layer], ln_rstd[:, layer], ALU.mult)
                gp.drain()
                for b in range(NB):
                    last = nc.gpsimd.tensor_scalar(dst[:, b], src[:, b], ln_rstd[:, layer, b:b + 1], ln_shift[:, layer, b:b + 1],
                                                   ALU.mult, ALU.add)
                last.then_inc(finished, 1)

            def split_xt(base, c):
                if here(base, c):
                    gp.wait_ge(a_xt, done(base, c))
                    nc.gpsimd.tensor_tensor(xt_lo[:, c % 2], xt[:], xt_hi[:, c % 2].bitcast(f32),
                                            ALU.subtract).then_inc(g_xt, 1)

            def iteration(base, k):
                if here(base, k):
                    gp.wait_ge(v_deg, done(base, k))
                    if here(base, k - 1):
                        gp.wait_ge(p_bt, done(base, k - 1))
                    nc.gpsimd.tensor_tensor(badj[:], adj[:, k % 2],
                                            deg_inv[:, :, None].broadcast_to([P, NB, N]), ALU.mult).then_inc(g_badj, 1)
                if here(base, k - 2):
                    gp.wait_ge(v_mv2, done(base, k - 2))
                    if here(base, k - 4):
                        gp.wait_ge(s_res[k % 2], landed(base, k - 4))
                    normalise(1, mv2, y2[:], res[:, k % 2], g_res)
                if k > -1:
                    split_xt(base, k + 2)
                if here(base, k + 1):
                    gp.wait_ge(v_inv, done(base, k + 1))
                    nc.gpsimd.tensor_tensor(trans[:], trans[:], row_inv[:, :, None].broadcast_to([P, NB, N]),
                                            ALU.mult).then_inc(g_t, 1)
                if here(base, k):
                    gp.wait_ge(v_mv1, done(base, k))
                    normalise(0, mv1, y1[:], x1[:, k % 2], g_x1)

            split_xt(0, 0)
            split_xt(0, 1)
            for k in BEFORE[1:]:
                iteration(0, k)
            with gp.Fori(0, LOOPED // UNROLL) as group:
                for k in range(FIRST_LOOPED, FIRST_LOOPED + UNROLL):
                    iteration(group * UNROLL, k)
            for k in AFTER:
                iteration(0, k)

        @block.scalar
        def _(act):
            def high(dst, src, finished):
                nc.scalar.activation(dst, src, ACT.Copy).then_inc(finished, 1)

            act.dma_start(wv[:], wv_in.rearrange("(b p) d -> p b d", p=P)).then_inc(s_wv, 16)
            act.dma_start(aw[:], aw_in.rearrange("(h d) one -> one h d", d=D).broadcast_to([P, 2, D])).then_inc(s_wv, 16)
            act.dma_start(bv[:], bv_in.rearrange("(one d) -> one d", one=1).broadcast_to([P, D])).then_inc(s_const_in, 16)
            act.dma_start(ab[:], ab_in.rearrange("(one d) -> one d", one=1).broadcast_to([P, 1])).then_inc(s_const_in, 16)
            act.dma_start(bk[:], bk_in.rearrange("(one k) d -> one k d", one=1).broadcast_to([P, 3, D])).then_inc(s_bk, 16)

            def exponentials(base, c):
                act.wait_ge(p_sj, done(base, c))
                for b in range(NB):
                    nc.scalar.activation(steep[:, b].rearrange("p (j q) -> p j q", q=P), sj_ps, ACT.Exp,
                                         bias=scores[:, b, SI:SI + 1])
                    last = nc.scalar.activation(gentle[:, b].rearrange("p (j q) -> p j q", q=P), sj_ps, ACT.Exp,
                                                bias=scores[:, b, SI_SLOPED:SI_SLOPED + 1], scale=SLOPE)
                last.then_inc(a_exp, 1)

            def degrees(base, c):
                if here(base, c):
                    act.wait_ge(s_adj[c % 2], landed(base, c))
                    for b in range(NB):
                        last = nc.scalar.activation(deg_scratch[:, b], adj[:, c % 2, b], ACT.Copy,
                                                    accum_out=deg[:, b:b + 1])
                    last.then_inc(a_deg, 1)

            def high_xt(base, c):
                if here(base, c):
                    act.wait_ge(v_xt, done(base, c))
                    high(xt_hi[:, c % 2], xt[:], a_xt)

            def high_u(base, c):
                if here(base, c):
                    act.wait_ge(p_u, done(base, c))
                    high(u_hi[:, c % 2], u_ps[:, :, 0:D], a_u)

            def iteration(base, k):
                if here(base, k):
                    act.wait_ge(p_tt, done(base, k))
                    high(tt_hi[:], tb_ps[:], a_tt)
                if k != 0:
                    high_u(base, k + 1)
                else:
                    exponentials(base, 1)
                if here(base, k - 1):
                    act.wait_ge(p_x1t, done(base, k - 1))
                    high(x1t_hi[:], ta_ps[:], a_x1t)
                if here(base, k):
                    act.wait_ge(p_v, done(base, k))
                    high(v_hi[:], v_ps, a_v)
                    act.wait_ge(p_bt, done(base, k))
                    high(bt_hi[:, k % 2], tb_ps[:], a_bt)
                if here(base, k + 1) and k != 0:
                    exponentials(base, k + 1)
                high_xt(base, k + 2)
                if here(base, k - 1):
                    for b in range(NB):
                        act.wait_ge(p_g, done_block(base, k - 1, b))
                        high(g_hi[:, b], g_ps[:, b], a_g)
                degrees(base, k + 1)

            act.wait_ge(s_wk[2], 16)
            high(w2_hi[:, :, 0:D], wk[:, 2], s_whi)
            high_xt(0, 0)
            act.wait_ge(s_cols, 1)
            high(w2_hi[:, :, D:D + COLS], w2s[:], s_whi)
            degrees(0, 0)
            act.wait_ge(s_wk[1], 16)
            high(w10_hi[:, :, 0:D], wk[:, 1], s_whi)
            act.wait_ge(g_xt, done(0, 0))
            high_xt(0, 1)
            high_u(0, 0)
            exponentials(0, 0)
            act.wait_ge(s_wk[0], 16)
            high(w10_hi[:, :, D:2 * D], wk[:, 0], s_whi)
            act.wait_ge(s_wt, 1)
            high(wax_hi[:, :, D:2 * D], v_ps, s_whi)
            high(wax_hi[:, :, 0:D], h_ps, s_whi)
            high_u(0, 1)
            for k in BEFORE[2:]:
                iteration(0, k)
            with act.Fori(0, LOOPED // UNROLL) as group:
                for k in range(FIRST_LOOPED, FIRST_LOOPED + UNROLL):
                    iteration(group * UNROLL, k)
            for k in AFTER:
                iteration(0, k)

        @block.vector
        def _(dve):
            def low(dst, src, hi, finished):
                nc.vector.tensor_tensor(dst, src, hi.bitcast(f32), ALU.subtract).then_inc(finished, 1)

            nc.vector.memset(w2s[:], 0.0).then_inc(s_parts, 1)
            nc.vector.memset(score_const[:], 0.0).then_inc(s_parts, 1)
            dve.wait_ge(s_parts, 2)
            dve.wait_ge(s_wv, 16 * 2)
            for b in range(DB):
                for col in (SJ, SI):
                    nc.vector.scalar_tensor_tensor(score_scratch[:, 2 * b + col], wv[:, b], 1.0, aw[:, col], ALU.mult,
                                                   ALU.mult, accum_out=w2s[:, b, col:col + 1]).then_inc(s_parts, 1)
            dve.wait_ge(s_parts, 2 + 4)
            nc.vector.tensor_scalar(w2s[:, :, SI_SLOPED], w2s[:, :, SI], SLOPE, None, ALU.mult).then_inc(s_cols, 1)

            def score_constant():
                dve.wait_ge(s_const_in, 16 * 2)
                for col in (SJ, SI):
                    nc.vector.scalar_tensor_tensor(score_scratch[:, 4 + col], bv[:], 1.0, aw[:, col], ALU.mult,
                                                   ALU.mult, accum_out=const_parts[:, col:col + 1]).then_inc(s_parts, 1)
                dve.wait_ge(s_parts, 2 + 6)
                nc.vector.scalar_tensor_tensor(score_const[:, SI:SI + 1], const_parts[:, 0:1], ab[:],
                                               const_parts[:, 1:2], ALU.add, ALU.add).then_inc(s_const, 1)
                dve.wait_ge(s_const, 1)
                nc.vector.tensor_scalar(score_const[:, SI_SLOPED:SI_SLOPED + 1], score_const[:, SI:SI + 1], SLOPE,
                                        None, ALU.mult).then_inc(s_const, 1)
                dve.wait_ge(s_const, 2)

            def summed_biases():
                dve.wait_ge(s_bk, 16)
                nc.vector.tensor_tensor(bias01[:], bk[:, 0], bk[:, 1], ALU.add).then_inc(s_bias01, 1)
                dve.wait_ge(s_bias01, 1)
                nc.vector.tensor_tensor(bias[:], bias01[:], bk[:, 2], ALU.add).then_inc(s_bias, 1)
                dve.wait_ge(s_bias, 1)

            def degrees(base, c):
                if here(base, c):
                    if here(base, c - 1):
                        dve.wait_ge(g_badj, done(base, c - 1))
                    dve.wait_ge(a_deg, done(base, c))
                    nc.vector.tensor_scalar(deg_inv[:], deg[:], DEG_EPS, None, ALU.max).then_inc(v_degc, 1)
                    dve.wait_ge(v_degc, done(base, c))
                    nc.vector.reciprocal(deg_inv[:], deg_inv[:]).then_inc(v_deg, 1)

            def split_u(base, c):
                if here(base, c):
                    dve.wait_ge(a_u, done(base, c))
                    nc.vector.tensor_tensor(scores[:], u_ps[:, :, D:D + COLS],
                                            score_const[:, None, :].broadcast_to([P, NB, COLS]), ALU.add)
                    low(u_lo[:, c % 2], u_ps[:, :, 0:D], u_hi[:, c % 2], v_u)

            def transpose_x(base, c):
                if here(base, c):
                    if here(base, c - 1):
                        dve.wait_ge(g_xt, done(base, c - 1))
                    dve.wait_ge(s_xs[c % 2], landed(base, c, P // TILE))
                    nc.vector.transpose(xt[:].rearrange("p d n -> p (d n)"),
                                        xs[:, c % 2].rearrange("p d q b -> p (d q b)")).then_inc(v_xt, 1)

            def larger_exponential(base, c):
                if here(base, c):
                    dve.wait_ge(a_exp, done(base, c))
                    nc.vector.tensor_tensor(steep[:], steep[:], gentle[:], ALU.max).then_inc(v_exp, 1)

            def edge_weights(base, c):
                if here(base, c):
                    dve.wait_ge(v_exp, done(base, c))
                    dve.wait_ge(s_adj[c % 2], landed(base, c))
                    for b in range(NB):
                        last = nc.vector.scalar_tensor_tensor(trans[:, b], adj[:, c % 2, b], 1.0, steep[:, b],
                                                              ALU.mult, ALU.mult, accum_out=row_sum[:, b:b + 1])
                    last.then_inc(v_alpha, 1)

            def row_inverse(base, c):
                if here(base, c):
                    dve.wait_ge(v_alpha, done(base, c))
                    nc.vector.tensor_scalar(row_inv[:], row_sum[:], SUM_EPS, None, ALU.add).then_inc(v_sum, 1)
                    dve.wait_ge(v_sum, done(base, c))
                    nc.vector.reciprocal(row_inv[:], row_inv[:]).then_inc(v_inv, 1)

            def statistics(base, c, y, written, bn, mv, finished):
                dve.wait_ge(written, done(base, c))
                for b in range(NB):
                    nc.vector.bn_stats(bn[:, b], y[:, b])
                dve.drain()
                for b in range(NB):
                    last = nc.vector.bn_aggr(mv[:, b], bn[:, b])
                last.then_inc(finished, 1)

            def iteration(base, k):
                degrees(base, k)
                if here(base, k - 2):
                    dve.wait_ge(p_o, done(base, k - 2))
                    if here(base, k - 3):
                        dve.wait_ge(g_res, done(base, k - 3))
                    nc.vector.scalar_tensor_tensor(y2[:], o_ps, 0.0, x1[:, (k - 2) % 2], ALU.max,
                                                   ALU.add).then_inc(v_y2, 1)
                    statistics(base, k - 2, y2[:], v_y2, bn2[:], mv2[:], v_mv2)
                if here(base, k):
                    dve.wait_ge(a_tt, done(base, k))
                    low(tt_lo[:], tb_ps[:], tt_hi[:], v_tt)
                if k != 0:
                    split_u(base, k + 1)
                else:
                    larger_exponential(base, 1)
                    edge_weights(base, 1)
                if here(base, k - 1):
                    dve.wait_ge(a_x1t, done(base, k - 1))
                    low(x1t_lo[:], ta_ps[:], x1t_hi[:], v_x1t)
                if here(base, k):
                    dve.wait_ge(a_v, done(base, k))
                    low(v_lo[:], v_ps, v_hi[:], v_v)
                    dve.wait_ge(a_bt, done(base, k))
                    low(bt_lo[:, k % 2], tb_ps[:], bt_hi[:, k % 2], v_bt)
                transpose_x(base, k + 2)
                if k != 0:
                    larger_exponential(base, k + 1)
                if here(base, k - 1):
                    for b in range(NB):
                        dve.wait_ge(a_g, done_block(base, k - 1, b))
                        low(g_lo[:, b], g_ps[:, b], g_hi[:, b], v_g)
                if k != 0:
                    edge_weights(base, k + 1)
                if here(base, k):
                    dve.wait_ge(p_h, done(base, k))
                    nc.vector.tensor_tensor(y1[:], h_ps, bias[:, None, :].broadcast_to([P, NB, D]),
                                            ALU.add).then_inc(v_hb, 1)
                row_inverse(base, k + 1)
                if here(base, k):
                    dve.wait_ge(v_hb, done(base, k))
                    dve.wait_ge(s_x[k % 2], landed(base, k))
                    nc.vector.scalar_tensor_tensor(y1[:], y1[:], 0.0, x[:, k % 2], ALU.max,
                                                   ALU.add).then_inc(v_y1, 1)
                    statistics(base, k, y1[:], v_y1, bn1[:], mv1[:], v_mv1)

            transpose_x(0, 0)
            dve.wait_ge(s_whi, W2)
            low(w2_lo[:, :, 0:D], wk[:, 2], w2_hi[:, :, 0:D], s_wlo)
            dve.wait_ge(s_whi, W2_COLS)
            low(w2_lo[:, :, D:D + COLS], w2s[:], w2_hi[:, :, D:D + COLS], s_wlo)
            score_constant()
            dve.wait_ge(s_whi, W1)
            low(w10_lo[:, :, 0:D], wk[:, 1], w10_hi[:, :, 0:D], s_wlo)
            transpose_x(0, 1)
            split_u(0, 0)
            larger_exponential(0, 0)
            edge_weights(0, 0)
            row_inverse(0, 0)
            dve.wait_ge(s_whi, W0)
            low(w10_lo[:, :, D:2 * D], wk[:, 0], w10_hi[:, :, D:2 * D], s_wlo)
            dve.wait_ge(s_whi, WA)
            low(wax_lo[:, :, D:2 * D], v_ps, wax_hi[:, :, D:2 * D], s_wlo)
            low(wax_lo[:, :, 0:D], h_ps, wax_hi[:, :, 0:D], s_wlo)
            split_u(0, 1)
            summed_biases()
            for k in BEFORE[2:]:
                iteration(0, k)
            with dve.Fori(0, LOOPED // UNROLL) as group:
                for k in range(FIRST_LOOPED, FIRST_LOOPED + UNROLL):
                    iteration(group * UNROLL, k)
            for k in AFTER:
                iteration(0, k)

        @block.tensor
        def _(pe):
            def product(dst, left, right, b, first):
                left_hi, left_lo = left
                right_hi, right_lo = right
                rows = slice(b * P, (b + 1) * P)
                for lh, rh in ((left_hi, right_lo), (left_lo, right_hi), (left_hi, right_hi)):
                    for kb in range(2):
                        last = nc.tensor.matmul(dst, lh[:, kb, rows], rh[:, kb], start=first, stop=True,
                                                skip_group_check=True)
                        first = False
                return last

            def transposed(dst, src):
                for c in range(2):
                    for r in range(2):
                        last = nc.tensor.transpose(dst[:, c, r * P:(r + 1) * P], src[:, r, c * P:(c + 1) * P],
                                                   ident[:])
                return last

            def u_product(base, c):
                if here(base, c):
                    pe.wait_ge(g_xt, done(base, c))
                    if here(base, c - 1):
                        pe.wait_ge(a_exp, done(base, c - 1))
                    for b in range(NB):
                        last = product(u_ps[:, b, 0:D + COLS], (xt_hi[:, c % 2], xt_lo[:, c % 2]), (w2_hi, w2_lo), b,
                                       True)
                    last.then_inc(p_u, 1)

            def broadcast_sj(base, c):
                if here(base, c):
                    pe.wait_ge(v_u, done(base, c))
                    for b in range(NB):
                        last = nc.tensor.transpose(sj_ps[:, b], scores[:, b, SJ:SJ + 1].broadcast_to([P, P]), ident[:])
                    last.then_inc(p_sj, 1)

            def transpose_b(base, c):
                if here(base, c):
                    pe.wait_ge(g_badj, done(base, c))
                    transposed(tb_ps, badj).then_inc(p_bt, 1)

            def transpose_t(base, c):
                if here(base, c):
                    pe.wait_ge(g_t, done(base, c))
                    if here(base, c - 1):
                        pe.wait_ge(v_bt, done(base, c - 1))
                    transposed(tb_ps, trans).then_inc(p_tt, 1)

            def iteration(base, k):
                if here(base, k):
                    if here(base, k - 1):
                        pe.wait_ge(v_hb, done(base, k - 1))
                    for b in range(NB):
                        product(vh_ps[:, b], (xt_hi[:, k % 2], xt_lo[:, k % 2]), (w10_hi, w10_lo), b, True)
                        if b == 0:
                            transpose_t(base, k)
                if k != 0:
                    u_product(base, k + 1)
                else:
                    broadcast_sj(base, 1)
                if here(base, k - 1):
                    pe.wait_ge(g_x1, done(base, k - 1))
                    transposed(ta_ps, x1[:, (k - 1) % 2]).then_inc(p_x1t, 1)
                if here(base, k):
                    pe.wait_ge(v_tt, done(base, k))
                    for b in range(NB):
                        last = product(v_ps[:, b], (tt_hi, tt_lo), (u_hi[:, k % 2], u_lo[:, k % 2]), b, False)
                    last.then_inc(p_v, 1)
                if k != 0:
                    broadcast_sj(base, k + 1)
                transpose_b(base, k)
                if here(base, k - 1):
                    if here(base, k - 2):
                        pe.wait_ge(v_y2, done(base, k - 2))
                    pe.wait_ge(v_x1t, done(base, k - 1))
                    for b in range(NB):
                        product(go_ps[:, b], (x1t_hi, x1t_lo), (wax_hi, wax_lo), b, True).then_inc(p_g, 1)
                if here(base, k):
                    pe.wait_ge(v_v, done(base, k))
                    for b in range(NB):
                        last = product(h_ps[:, b], (tt_hi, tt_lo), (v_hi, v_lo), b, False)
                    last.then_inc(p_h, 1)
                if here(base, k - 1):
                    pe.wait_ge(v_g, done_block(base, k - 1, NB - 1))
                    for b in range(NB):
                        last = product(o_ps[:, b], (bt_hi[:, (k - 1) % 2], bt_lo[:, (k - 1) % 2]), (g_hi, g_lo), b,
                                       False)
                    last.then_inc(p_o, 1)

            pe.wait_ge(s_ident, 1)
            pe.wait_ge(s_wlo, W2_COLS)
            u_product(0, 0)
            pe.wait_ge(s_wcat, 16)
            transposed(v_ps, wcat[:, :, 0:D])
            transposed(h_ps, wcat[:, :, D:2 * D]).then_inc(s_wt, 1)
            broadcast_sj(0, 0)
            u_product(0, 1)
            pe.wait_ge(s_wlo, WA)
            for k in BEFORE[2:]:
                iteration(0, k)
            with pe.Fori(0, LOOPED // UNROLL) as group:
                for k in range(FIRST_LOOPED, FIRST_LOOPED + UNROLL):
                    iteration(group * UNROLL, k)
            for k in AFTER:
                iteration(0, k)


_INS = ["x", "adj", "L0_gnn_Wv", "L0_gnn_bv", "L0_gnn_aw", "L0_gnn_ab", "L0_gnn_Wk", "L0_gnn_bk", "L1_gnn_W"]


def kernel(**inputs):
    import numpy as np
    import concourse.bacc as bacc
    from concourse.bass_utils import run_bass_kernel_spmd

    nc = bacc.Bacc("TRN2", target_bir_lowering=False, num_devices=1)
    arrays, args = {}, []
    for name in _INS:
        a = np.ascontiguousarray(inputs[name])
        arrays[f"in_{name}"] = a
        args.append(nc.dram_tensor(f"in_{name}", a.shape, mybir.dt.from_np(a.dtype), kind="ExternalInput").ap())
    out = nc.dram_tensor("result", arrays["in_x"].shape, mybir.dt.float32, kind="ExternalOutput").ap()
    build(nc, *args, out)
    r = run_bass_kernel_spmd(nc, [arrays], core_ids=[0])
    return r.results[0]["result"]
```

```python
import concourse.bass as bass
from concourse import mybir
from contextlib import ExitStack


def build(nc, x_in, adj_in, wv_in, bv_in, aw_in, ab_in, wk_in, bk_in, w1_in, out):
    f32, f32r = mybir.dt.float32, mybir.dt.float32r
    ALU, ACT, AX = mybir.AluOpType, mybir.ActivationFunctionType, mybir.AxisListType

    GRAPHS, N, D = x_in.shape
    P = 128
    NB = N // P
    DB = D // P
    LN_EPS, SUM_EPS, DEG_EPS, SLOPE = 1e-5, 1e-12, 1e-6, 0.2
    COLS = 4
    SJ, SI, SI_SLOPED = 0, 1, 2
    TILE = 32
    UNROLL = 4
    TILED = 2
    LAST = GRAPHS - 1
    FIRST_LOOPED = 2
    LOOPED = (GRAPHS - 2 - FIRST_LOOPED) // UNROLL * UNROLL
    AFTER = range(FIRST_LOOPED + LOOPED, LAST)
    CLOCK_TRANSPOSES = 8, 8, 4

    x_rows = x_in.rearrange("g (b p) d -> g p b d", p=P)
    x_tiles = x_in.rearrange("g (q a) (d c b) -> g c a d q b", a=TILE, b=TILE, c=P // TILE)
    adj_rows = adj_in.rearrange("g (b p) d -> g p b d", p=P)
    out_rows = out.rearrange("g (b p) d -> g p b d", p=P)


    def here(base, c):
        return not isinstance(base, int) or 0 <= c < GRAPHS

    def done(base, c):
        return base + (c + 1)

    def done_tiled(base, c):
        return base + (c - TILED + 1)

    def landed_tiles(base, c):
        return landed(base, c - TILED, P // TILE)

    def done_block(base, c, b):
        return base * NB + (c * NB + b + 1)

    def landed(base, c, transfers=1):
        return base * (8 * transfers) + 16 * transfers * (c // 2 + 1)

    ctx = ExitStack()
    with ctx:
        def sb(name, shape, dt=f32):
            return ctx.enter_context(nc.sbuf_tensor(name, shape, dt))

        def sem(name):
            return ctx.enter_context(nc.semaphore(name))

        x = sb("x", [P, 2, NB, D])
        xs = sb("xs", [P, 2, DB, N // TILE, TILE])
        xt = sb("xt", [P, DB, N])
        adj = sb("adj", [P, 2, NB, N])
        xt_hi, xt_lo = sb("xt_hi", [P, 2, DB, N], f32r), sb("xt_lo", [P, 2, DB, N], f32r)
        u_hi, u_lo = sb("u_hi", [P, 2, NB, D], f32r), sb("u_lo", [P, 2, NB, D], f32r)
        v_hi, v_lo = sb("v_hi", [P, NB, D], f32r), sb("v_lo", [P, NB, D], f32r)
        tt_hi, tt_lo = sb("tt_hi", [P, NB, N], f32r), sb("tt_lo", [P, NB, N], f32r)
        bt_hi, bt_lo = sb("bt_hi", [P, 2, NB, N], f32r), sb("bt_lo", [P, 2, NB, N], f32r)
        x1t_hi, x1t_lo = sb("x1t_hi", [P, DB, N], f32r), sb("x1t_lo", [P, DB, N], f32r)
        g_hi, g_lo = sb("g_hi", [P, NB, D], f32r), sb("g_lo", [P, NB, D], f32r)
        steep, gentle = sb("steep", [P, NB, N]), sb("gentle", [P, NB, N])
        trans = sb("trans", [P, NB, N])
        badj = sb("badj", [P, NB, N])
        y1 = sb("y1", [P, NB, D])
        x1 = sb("x1", [P, 2, NB, D])
        y2 = sb("y2", [P, NB, D])
        res = sb("res", [P, 2, NB, D])
        scores = sb("scores", [P, NB, COLS])
        row_sum, row_inv = sb("row_sum", [P, NB]), sb("row_inv", [P, NB])
        deg, deg_inv = sb("deg", [P, NB]), sb("deg_inv", [P, NB])
        deg_scratch = sb("deg_scratch", [P, NB, N])
        bn1, bn2 = sb("bn1", [P, NB, 6]), sb("bn2", [P, NB, 6])
        mv1, mv2 = sb("mv1", [P, NB, 2]), sb("mv2", [P, NB, 2])
        ln_var, ln_rstd, ln_shift = (sb(f"ln_{name}", [P, 2, NB]) for name in ("var", "rstd", "shift"))

        w2_hi, w2_lo = sb("w2_hi", [P, DB, D + COLS], f32r), sb("w2_lo", [P, DB, D + COLS], f32r)
        w10_hi, w10_lo = sb("w10_hi", [P, DB, 2 * D], f32r), sb("w10_lo", [P, DB, 2 * D], f32r)
        wax_hi, wax_lo = sb("wax_hi", [P, DB, 2 * D], f32r), sb("wax_lo", [P, DB, 2 * D], f32r)
        wk = sb("wk", [P, 3, DB, D])
        wv = sb("wv", [P, DB, D])
        wcat = sb("wcat", [P, D // P, 2 * D])
        aw = sb("aw", [P, 2, D])
        bv, ab, bk = sb("bv", [P, D]), sb("ab", [P, 1]), sb("bk", [P, 3, D])
        bias01, bias = sb("bias01", [P, D]), sb("bias", [P, D])
        w2s = sb("w2s", [P, DB, COLS])
        score_scratch = sb("score_scratch", [P, 6, D])
        const_parts, score_const = sb("const_parts", [P, 3]), sb("score_const", [P, COLS])
        minus_half, minus_one, ln_eps = sb("minus_half", [P, NB]), sb("minus_one", [P, NB]), sb("ln_eps", [P, NB])
        ident = sb("ident", [P, P])

        def bank(name, shape):
            return ctx.enter_context(nc.psum_tensor(name, shape, f32))

        u_ps = bank("u_ps", [P, 2, 512])
        vh_ps = bank("vh_ps", [P, 2, 512])
        go_ps = bank("go_ps", [P, 2, 512])
        ta_ps = bank("ta_ps", [P, 2, 256])
        tb_ps = bank("tb_ps", [P, 2, 256])
        sj_ps = u_ps[:, :, 384:512]
        v_ps, h_ps = vh_ps[:, :, 0:D], vh_ps[:, :, D:2 * D]
        g_ps, o_ps = go_ps[:, :, 0:D], go_ps[:, :, D:2 * D]

        s_x = [sem(f"s_x{i}") for i in range(2)]
        s_xs = [sem(f"s_xs{i}") for i in range(2)]
        s_adj = [sem(f"s_adj{i}") for i in range(2)]
        s_res = [sem(f"s_res{i}") for i in range(2)]
        s_last = sem("s_last")
        s_wk = [sem(f"s_wk{i}") for i in range(3)]
        s_wcat, s_wv, s_const_in, s_bk = sem("s_wcat"), sem("s_wv"), sem("s_const_in"), sem("s_bk")
        s_ident0, s_ident, s_half = sem("s_ident0"), sem("s_ident"), sem("s_half")
        s_wt = sem("s_wt")
        a_w = sem("a_w")
        W2, W2_COLS, W1, W0, WX, WA = range(1, 7)
        g_w, v_w = sem("g_w"), sem("v_w")
        s_cols, s_parts, s_const = sem("s_cols"), sem("s_parts"), sem("s_const")
        s_bias01, s_bias = sem("s_bias01"), sem("s_bias")
        p_u, p_sj, p_tt, p_bt = sem("p_u"), sem("p_sj"), sem("p_tt"), sem("p_bt")
        p_v, p_h, p_x1t, p_g, p_o = sem("p_v"), sem("p_h"), sem("p_x1t"), sem("p_g"), sem("p_o")
        a_xt, a_u, a_tt, a_bt = sem("a_xt"), sem("a_u"), sem("a_tt"), sem("a_bt")
        a_v, a_x1t, a_g, a_exp, a_deg = sem("a_v"), sem("a_x1t"), sem("a_g"), sem("a_exp"), sem("a_deg")
        p_xt, v_xt, xt_split = sem("p_xt"), sem("v_xt"), sem("xt_split")
        v_u, v_tt, v_bt = sem("v_u"), sem("v_tt"), sem("v_bt")
        v_v, v_x1t, v_g = sem("v_v"), sem("v_x1t"), sem("v_g")
        v_degc, v_deg = sem("v_degc"), sem("v_deg")
        v_alpha, v_sum, v_inv, v_exp = sem("v_alpha"), sem("v_sum"), sem("v_inv"), sem("v_exp")
        p_vh0 = sem("p_vh0")
        v_scores = sem("v_scores")
        v_hb, v_y1, v_mv1 = sem("v_hb"), sem("v_y1"), sem("v_mv1")
        v_y2, v_mv2 = sem("v_y2"), sem("v_mv2")
        g_t, g_badj, g_x1, g_res = sem("g_t"), sem("g_badj"), sem("g_x1"), sem("g_res")
        g_scales, v_x1, v_res = sem("g_scales"), sem("v_x1"), sem("v_res")

        block = ctx.enter_context(nc.Block())

        @block.sync
        def _(sp):
            def load_x(base, c):
                if here(base, c):
                    if here(base, c - 2):
                        sp.wait_ge(v_y1, done(base, c - 2))
                    sp.dma_start(x[:, c % 2], x_rows[base + c]).then_inc(s_x[c % 2], 16)

            def load_tiles(base, c):
                if here(base, c):
                    if here(base, c - 2 - TILED):
                        sp.wait_ge(v_xt, done_tiled(base, c - 2))
                    for t in range(P // TILE):
                        sp.dma_start(xs[t * TILE:(t + 1) * TILE, c % 2], x_tiles[base + c, t]).then_inc(s_xs[c % 2], 16)

            def load_adj(base, c):
                if not here(base, c):
                    return
                if here(base, c - 2):
                    sp.wait_ge(v_alpha, done(base, c - 2))
                    sp.wait_ge(g_badj, done(base, c - 2))
                sp.dma_start(adj[:, c % 2], adj_rows[base + c]).then_inc(s_adj[c % 2], 16)

            def store(base, c):
                if here(base, c):
                    sp.wait_ge(g_res, done(base, c))
                    sp.dma_start(out_rows[base + c], res[:, c % 2]).then_inc(s_res[c % 2], 16)

            def iteration(base, k):
                load_tiles(base, k + 2)
                load_adj(base, k + 2)
                load_x(base, k + 1)
                store(base, k - 2)

            def load_wk(i):
                sp.dma_start(wk[:, i], wk_in[i].rearrange("(b p) d -> p b d", p=P)).then_inc(s_wk[i], 16)

            load_x(0, 0)
            load_wk(2)
            load_x(0, 1)
            sp.dma_start(bv[:], bv_in.rearrange("(one d) -> one d", one=1).broadcast_to([P, D])).then_inc(s_const_in, 16)
            sp.dma_start(ab[:], ab_in.rearrange("(one d) -> one d", one=1).broadcast_to([P, 1])).then_inc(s_const_in, 16)
            load_wk(1)
            load_wk(0)
            load_adj(0, 0)
            load_tiles(0, 2)
            sp.dma_start(wcat[:], w1_in.rearrange("(b p) f -> p b f", p=P)).then_inc(s_wcat, 16)
            load_adj(0, 1)
            sp.dma_start(bk[:], bk_in.rearrange("(one k) d -> one k d", one=1).broadcast_to([P, 3, D])).then_inc(s_bk, 16)
            load_adj(0, 2)
            iteration(0, 1)
            with sp.Fori(0, LOOPED // UNROLL) as group:
                for k in range(FIRST_LOOPED, FIRST_LOOPED + UNROLL):
                    iteration(group * UNROLL, k)
            for k in AFTER:
                iteration(0, k)
            store(0, LAST - 2)
            store(0, LAST - 1)
            sp.wait_ge(g_res, done(0, LAST))
            sp.dma_start(out_rows[LAST, :, 0], res[:, LAST % 2, 0]).then_inc(s_last, 16)
            sp.wait_ge(s_res[(LAST - 1) % 2], landed(0, LAST - 1))
            sp.wait_ge(s_res[LAST % 2], landed(0, LAST - 2))
            sp.wait_ge(s_last, 16 * NB)

        @block.gpsimd
        def _(gp):
            nc.gpsimd.memset(ident[:], 0.0).then_inc(s_ident0, 1)
            nc.gpsimd.memset(minus_half[:], -0.5).then_inc(s_half, 1)
            nc.gpsimd.memset(minus_one[:], -1.0).then_inc(s_half, 1)
            nc.gpsimd.memset(ln_eps[:], LN_EPS).then_inc(s_half, 1)
            gp.wait_ge(s_ident0, 1)
            nc.gpsimd.affine_select(out=ident[:], in_=ident[:], compare_op=ALU.not_equal, fill=1.0, base=0,
                                    pattern=[[-1, P]], channel_multiplier=1).then_inc(s_ident, 1)
            gp.wait_ge(s_half, 3)

            def row_scales(layer, mv):
                nc.gpsimd.tensor_tensor(ln_var[:, layer], mv[:, :, 1], ln_eps[:], ALU.add)
                nc.gpsimd.tensor_tensor(ln_shift[:, layer], mv[:, :, 0], minus_one[:], ALU.mult)
                gp.drain()
                nc.gpsimd.tensor_tensor(ln_rstd[:, layer], ln_var[:, layer], minus_half[:], ALU.pow)
                gp.drain()
                return nc.gpsimd.tensor_tensor(ln_shift[:, layer], ln_shift[:, layer], ln_rstd[:, layer], ALU.mult)

            def normalise(layer, mv, src, dst, finished):
                row_scales(layer, mv)
                gp.drain()
                for b in range(NB):
                    last = nc.gpsimd.tensor_scalar(dst[:, b], src[:, b], ln_rstd[:, layer, b:b + 1], ln_shift[:, layer, b:b + 1],
                                                   ALU.mult, ALU.add)
                last.then_inc(finished, 1)

            def normalise_block0(nth, src, dst, finished):
                row_scales(0, mv1).then_inc(g_scales, 1)
                gp.wait_ge(g_scales, nth)
                nc.gpsimd.tensor_scalar(dst[:, 0], src[:, 0], ln_rstd[:, 0, 0:1], ln_shift[:, 0, 0:1],
                                        ALU.mult, ALU.add).then_inc(finished, 1)

            def split_xt(base, c):
                if here(base, c):
                    gp.wait_ge(a_xt, done(base, c))
                    nc.gpsimd.tensor_tensor(xt_lo[:, c % 2], xt[:], xt_hi[:, c % 2].bitcast(f32),
                                            ALU.subtract).then_inc(xt_split, 1)

            def scale_t(base, c):
                if here(base, c):
                    gp.wait_ge(v_inv, done(base, c))
                    nc.gpsimd.tensor_tensor(trans[:], trans[:], row_inv[:, :, None].broadcast_to([P, NB, N]),
                                            ALU.mult).then_inc(g_t, 1)

            def make_b(base, c):
                if here(base, c):
                    gp.wait_ge(v_deg, done(base, c))
                    if here(base, c - 1):
                        gp.wait_ge(p_bt, done(base, c - 1))
                    nc.gpsimd.tensor_tensor(badj[:], adj[:, c % 2],
                                            deg_inv[:, :, None].broadcast_to([P, NB, N]), ALU.mult).then_inc(g_badj, 1)

            def normalise_first(base, c):
                gp.wait_ge(v_mv1, done(base, c))
                normalise(0, mv1, y1[:], x1[:, c % 2], g_x1)

            def normalise_second(base, c):
                if here(base, c):
                    gp.wait_ge(v_mv2, done(base, c))
                    if here(base, c - 2):
                        gp.wait_ge(s_res[c % 2], landed(base, c - 2))
                    normalise(1, mv2, y2[:], res[:, c % 2], g_res)

            def iteration(base, k):
                make_b(base, k)
                normalise_second(base, k - 2)
                split_xt(base, k + 2)
                scale_t(base, k + 1)
                normalise_first(base, k)

            for nth, lo, hi, part in ((W2, w2_lo, w2_hi, 2), (W1, w10_lo[:, :, 0:D], w10_hi[:, :, 0:D], 1),
                                      (W0, w10_lo[:, :, D:2 * D], w10_hi[:, :, D:2 * D], 0)):
                gp.wait_ge(a_w, nth)
                nc.gpsimd.tensor_tensor(lo[:, :, 0:D], wk[:, part], hi[:, :, 0:D].bitcast(f32),
                                        ALU.subtract).then_inc(g_w, 1)
            make_b(0, 0)
            scale_t(0, 0)
            split_xt(0, 2)
            scale_t(0, 1)
            make_b(0, 1)
            normalise_first(0, 0)
            split_xt(0, 3)
            scale_t(0, 2)
            normalise_first(0, 1)
            with gp.Fori(0, LOOPED // UNROLL) as group:
                for k in range(FIRST_LOOPED, FIRST_LOOPED + UNROLL):
                    iteration(group * UNROLL, k)
            for k in AFTER:
                iteration(0, k)
            make_b(0, LAST)
            normalise_second(0, LAST - 2)
            gp.wait_ge(v_mv1, done(0, LAST))
            normalise_block0(1, y1[:], x1[:, LAST % 2], g_x1)
            normalise_second(0, LAST - 1)
            gp.wait_ge(v_mv1, done(0, LAST) + 1)
            gp.wait_ge(s_res[LAST % 2], landed(0, LAST - 2))
            normalise_block0(2, y1[:], res[:, LAST % 2], g_res)

        @block.scalar
        def _(act):
            def high(dst, src, finished):
                nc.scalar.activation(dst, src, ACT.Copy).then_inc(finished, 1)

            act.dma_start(wv[:], wv_in.rearrange("(b p) d -> p b d", p=P)).then_inc(s_wv, 16)
            act.dma_start(aw[:], aw_in.rearrange("(h d) one -> one h d", d=D).broadcast_to([P, 2, D])).then_inc(s_wv, 16)

            def exponentials(base, c):
                if not here(base, c):
                    return
                act.wait_ge(p_sj, done(base, c))
                for b in range(NB):
                    nc.scalar.activation(steep[:, b].rearrange("p (j q) -> p j q", q=P), sj_ps, ACT.Exp,
                                         bias=scores[:, b, SI:SI + 1])
                    last = nc.scalar.activation(gentle[:, b].rearrange("p (j q) -> p j q", q=P), sj_ps, ACT.Exp,
                                                bias=scores[:, b, SI_SLOPED:SI_SLOPED + 1], scale=SLOPE)
                last.then_inc(a_exp, 1)

            def degrees(base, c):
                if here(base, c):
                    act.wait_ge(s_adj[c % 2], landed(base, c))
                    for b in range(NB):
                        last = nc.scalar.activation(deg_scratch[:, b], adj[:, c % 2, b], ACT.Copy,
                                                    accum_out=deg[:, b:b + 1])
                    last.then_inc(a_deg, 1)

            def high_xt(base, c):
                if here(base, c):
                    act.wait_ge(v_xt, done_tiled(base, c))
                    high(xt_hi[:, c % 2], xt[:], a_xt)

            def high_u(base, c):
                if here(base, c):
                    act.wait_ge(p_u, done(base, c))
                    high(u_hi[:, c % 2], u_ps[:, :, 0:D], a_u)

            def high_t(base, c):
                act.wait_ge(p_tt, done(base, c))
                high(tt_hi[:], tb_ps[:], a_tt)

            def high_v(base, c):
                act.wait_ge(p_v, done(base, c))
                high(v_hi[:], v_ps, a_v)

            def high_b(base, c, b_bank=tb_ps):
                act.wait_ge(p_bt, done(base, c))
                high(bt_hi[:, c % 2], b_bank[:], a_bt)

            def high_x1(base, c):
                act.wait_ge(p_x1t, done(base, c))
                high(x1t_hi[:], ta_ps[:], a_x1t)

            def high_g(base, c, g_bank=g_ps):
                for b in range(NB):
                    act.wait_ge(p_g, done_block(base, c, b))
                    high(g_hi[:, b], g_bank[:, b], a_g)

            def iteration(base, k):
                high_t(base, k)
                high_u(base, k + 1)
                high_x1(base, k - 1)
                high_v(base, k)
                high_b(base, k)
                exponentials(base, k + 1)
                high_g(base, k - 1)
                high_xt(base, k + 2)
                degrees(base, k + 1)

            def high_first_xt(c):
                act.wait_ge(p_xt, done(0, c))
                high(xt_hi[:, c], tb_ps[:], a_xt)

            high_first_xt(0)
            act.wait_ge(s_wk[2], 16)
            high(w2_hi[:, :, 0:D], wk[:, 2], a_w)
            act.wait_ge(s_cols, 1)
            high(w2_hi[:, :, D:D + COLS], w2s[:], a_w)
            high_first_xt(1)
            for half, part in enumerate((1, 0)):
                act.wait_ge(s_wk[part], 16)
                high(w10_hi[:, :, half * D:(half + 1) * D], wk[:, part], a_w)
            exponentials(0, 0)
            high_u(0, 0)
            degrees(0, 0)
            high_u(0, 1)
            high_t(0, 0)
            exponentials(0, 1)
            act.wait_ge(p_vh0, 1)
            high_xt(0, 2)
            high_b(0, 0, ta_ps)
            act.wait_ge(v_deg, done(0, 0))
            degrees(0, 1)
            high_v(0, 0)
            act.wait_ge(s_wt, 1)
            high(wax_hi[:, :, D:2 * D], g_ps, a_w)
            high(wax_hi[:, :, 0:D], o_ps, a_w)
            high_u(0, 2)
            high_t(0, 1)
            high_v(0, 1)
            high_b(0, 1)
            high_x1(0, 0)
            exponentials(0, 2)
            high_g(0, 0)
            high_xt(0, 3)
            degrees(0, 2)
            with act.Fori(0, LOOPED // UNROLL) as group:
                for k in range(FIRST_LOOPED, FIRST_LOOPED + UNROLL):
                    iteration(group * UNROLL, k)
            for k in AFTER:
                iteration(0, k)
            high_t(0, LAST)
            high_v(0, LAST)
            high_x1(0, LAST - 1)
            high_b(0, LAST)
            high_g(0, LAST - 1)
            for b, bank_of in enumerate((ta_ps, tb_ps)):
                act.wait_ge(p_x1t, done(0, LAST) + b)
                high(x1t_hi[:, b], bank_of[:, b], a_x1t)
            high_g(0, LAST, v_ps)
            act.wait_ge(v_res, 1)
            act.dma_start(out_rows[LAST, :, 1], res[:, LAST % 2, 1]).then_inc(s_last, 16)

        @block.vector
        def _(dve):
            def low(dst, src, hi, finished):
                nc.vector.tensor_tensor(dst, src, hi.bitcast(f32), ALU.subtract).then_inc(finished, 1)

            def score_columns():
                nc.vector.memset(w2s[:], 0.0).then_inc(s_parts, 1)
                nc.vector.memset(score_const[:], 0.0).then_inc(s_parts, 1)
                dve.wait_ge(s_parts, 2)
                dve.wait_ge(s_wv, 16 * 2)
                for b in range(DB):
                    for col in (SJ, SI):
                        nc.vector.scalar_tensor_tensor(score_scratch[:, 2 * b + col], wv[:, b], 1.0, aw[:, col],
                                                       ALU.mult, ALU.mult,
                                                       accum_out=w2s[:, b, col:col + 1]).then_inc(s_parts, 1)
                dve.wait_ge(s_parts, 2 + 4)
                nc.vector.tensor_scalar(w2s[:, :, SI_SLOPED], w2s[:, :, SI], SLOPE, None, ALU.mult).then_inc(s_cols, 1)

            def score_constant():
                dve.wait_ge(s_const_in, 16 * 2)
                for col in (SJ, SI):
                    nc.vector.scalar_tensor_tensor(score_scratch[:, 4 + col], bv[:], 1.0, aw[:, col], ALU.mult,
                                                   ALU.mult, accum_out=const_parts[:, col:col + 1]).then_inc(s_parts, 1)
                dve.wait_ge(s_parts, 2 + 6)
                nc.vector.scalar_tensor_tensor(score_const[:, SI:SI + 1], const_parts[:, 0:1], ab[:],
                                               const_parts[:, 1:2], ALU.add, ALU.add).then_inc(s_const, 1)
                dve.wait_ge(s_const, 1)
                nc.vector.tensor_scalar(score_const[:, SI_SLOPED:SI_SLOPED + 1], score_const[:, SI:SI + 1], SLOPE,
                                        None, ALU.mult).then_inc(s_const, 1)
                dve.wait_ge(s_const, 2)

            def summed_biases():
                dve.wait_ge(s_bk, 16)
                nc.vector.tensor_tensor(bias01[:], bk[:, 0], bk[:, 1], ALU.add).then_inc(s_bias01, 1)
                dve.wait_ge(s_bias01, 1)
                nc.vector.tensor_tensor(bias[:], bias01[:], bk[:, 2], ALU.add).then_inc(s_bias, 1)
                dve.wait_ge(s_bias, 1)

            def degrees(base, c):
                if here(base, c):
                    if here(base, c - 1):
                        dve.wait_ge(g_badj, done(base, c - 1))
                    dve.wait_ge(a_deg, done(base, c))
                    nc.vector.tensor_scalar(deg_inv[:], deg[:], DEG_EPS, None, ALU.max).then_inc(v_degc, 1)
                    dve.wait_ge(v_degc, done(base, c))
                    nc.vector.reciprocal(deg_inv[:], deg_inv[:]).then_inc(v_deg, 1)

            def score_sums():
                return nc.vector.tensor_tensor(scores[:], u_ps[:, :, D:D + COLS],
                                               score_const[:, None, :].broadcast_to([P, NB, COLS]), ALU.add)

            def split_u(base, c):
                if here(base, c):
                    dve.wait_ge(a_u, done(base, c))
                    score_sums()
                    low(u_lo[:, c % 2], u_ps[:, :, 0:D], u_hi[:, c % 2], v_u)

            def transpose_x(base, c):
                if here(base, c):
                    if here(base, c - 1 - TILED):
                        dve.wait_ge(xt_split, done(base, c - 1))
                    dve.wait_ge(s_xs[c % 2], landed_tiles(base, c))
                    nc.vector.transpose(xt[:].rearrange("p d n -> p (d n)"),
                                        xs[:, c % 2].rearrange("p d q b -> p (d q b)")).then_inc(v_xt, 1)

            def larger_exponential(base, c):
                if here(base, c):
                    dve.wait_ge(a_exp, done(base, c))
                    nc.vector.tensor_tensor(steep[:], steep[:], gentle[:], ALU.max).then_inc(v_exp, 1)

            def edge_weights(base, c):
                if here(base, c):
                    dve.wait_ge(v_exp, done(base, c))
                    dve.wait_ge(s_adj[c % 2], landed(base, c))
                    for b in range(NB):
                        last = nc.vector.scalar_tensor_tensor(trans[:, b], adj[:, c % 2, b], 1.0, steep[:, b],
                                                              ALU.mult, ALU.mult, accum_out=row_sum[:, b:b + 1])
                    last.then_inc(v_alpha, 1)

            def row_inverse(base, c):
                if here(base, c):
                    dve.wait_ge(v_alpha, done(base, c))
                    nc.vector.tensor_scalar(row_inv[:], row_sum[:], SUM_EPS, None, ALU.add).then_inc(v_sum, 1)
                    dve.wait_ge(v_sum, done(base, c))
                    nc.vector.reciprocal(row_inv[:], row_inv[:]).then_inc(v_inv, 1)

            def statistics(base, c, y, written, bn, mv, finished):
                dve.wait_ge(written, done(base, c))
                for b in range(NB):
                    nc.vector.bn_stats(bn[:, b], y[:, b])
                dve.drain()
                for b in range(NB):
                    last = nc.vector.bn_aggr(mv[:, b], bn[:, b])
                last.then_inc(finished, 1)

            def low_t(base, c):
                dve.wait_ge(a_tt, done(base, c))
                low(tt_lo[:], tb_ps[:], tt_hi[:], v_tt)

            def low_v(base, c):
                dve.wait_ge(a_v, done(base, c))
                low(v_lo[:], v_ps, v_hi[:], v_v)

            def low_b(base, c, b_bank=tb_ps):
                dve.wait_ge(a_bt, done(base, c))
                low(bt_lo[:, c % 2], b_bank[:], bt_hi[:, c % 2], v_bt)

            def low_x1(base, c):
                dve.wait_ge(a_x1t, done(base, c))
                low(x1t_lo[:], ta_ps[:], x1t_hi[:], v_x1t)

            def low_g(base, c, g_bank=g_ps):
                for b in range(NB):
                    dve.wait_ge(a_g, done_block(base, c, b))
                    low(g_lo[:, b], g_bank[:, b], g_hi[:, b], v_g)

            def add_bias(base, c):
                dve.wait_ge(p_h, done(base, c))
                nc.vector.tensor_tensor(y1[:], h_ps, bias[:, None, :].broadcast_to([P, NB, D]),
                                        ALU.add).then_inc(v_hb, 1)

            def add_x(base, c):
                dve.wait_ge(v_hb, done(base, c))
                dve.wait_ge(s_x[c % 2], landed(base, c))
                nc.vector.scalar_tensor_tensor(y1[:], y1[:], 0.0, x[:, c % 2], ALU.max, ALU.add).then_inc(v_y1, 1)
                statistics(base, c, y1[:], v_y1, bn1[:], mv1[:], v_mv1)

            def add_x1(base, c):
                if here(base, c):
                    dve.wait_ge(p_o, done(base, c))
                    if here(base, c - 1):
                        dve.wait_ge(g_res, done(base, c - 1))
                    nc.vector.scalar_tensor_tensor(y2[:], o_ps, 0.0, x1[:, c % 2], ALU.max, ALU.add).then_inc(v_y2, 1)
                    statistics(base, c, y2[:], v_y2, bn2[:], mv2[:], v_mv2)

            def iteration(base, k):
                degrees(base, k)
                add_x1(base, k - 2)
                low_t(base, k)
                split_u(base, k + 1)
                low_x1(base, k - 1)
                low_v(base, k)
                low_b(base, k)
                transpose_x(base, k + 2)
                larger_exponential(base, k + 1)
                low_g(base, k - 1)
                edge_weights(base, k + 1)
                add_bias(base, k)
                row_inverse(base, k + 1)
                add_x(base, k)

            def low_first_xt(c):
                dve.wait_ge(a_xt, done(0, c))
                low(xt_lo[:, c], tb_ps[:], xt_hi[:, c], xt_split)

            low_first_xt(0)
            score_columns()
            dve.wait_ge(a_w, W2_COLS)
            low(w2_lo[:, :, D:D + COLS], w2s[:], w2_hi[:, :, D:D + COLS], v_w)
            score_constant()
            low_first_xt(1)
            dve.wait_ge(p_u, done(0, 0))
            score_sums().then_inc(v_scores, 1)
            larger_exponential(0, 0)
            dve.wait_ge(a_u, done(0, 0))
            low(u_lo[:, 0], u_ps[:, :, 0:D], u_hi[:, 0], v_u)
            edge_weights(0, 0)
            row_inverse(0, 0)
            degrees(0, 0)
            split_u(0, 1)
            transpose_x(0, 2)
            low_t(0, 0)
            larger_exponential(0, 1)
            edge_weights(0, 1)
            row_inverse(0, 1)
            low_b(0, 0, ta_ps)
            summed_biases()
            low_v(0, 0)
            degrees(0, 1)
            dve.wait_ge(a_w, WA)
            low(wax_lo[:, :, D:2 * D], g_ps, wax_hi[:, :, D:2 * D], v_w)
            add_bias(0, 0)
            low(wax_lo[:, :, 0:D], o_ps, wax_hi[:, :, 0:D], v_w)
            split_u(0, 2)
            add_x(0, 0)
            low_t(0, 1)
            low_v(0, 1)
            low_b(0, 1)
            low_x1(0, 0)
            transpose_x(0, 3)
            larger_exponential(0, 2)
            low_g(0, 0)
            edge_weights(0, 2)
            add_bias(0, 1)
            row_inverse(0, 2)
            add_x(0, 1)
            with dve.Fori(0, LOOPED // UNROLL) as group:
                for k in range(FIRST_LOOPED, FIRST_LOOPED + UNROLL):
                    iteration(group * UNROLL, k)
            for k in AFTER:
                iteration(0, k)

            def last_statistics(written):
                for b in range(NB):
                    dve.wait_ge(written, done(0, LAST) + b)
                    nc.vector.bn_stats(bn1[:, b], y1[:, b])
                dve.drain()
                for b in range(NB):
                    last = nc.vector.bn_aggr(mv1[:, b], bn1[:, b])
                last.then_inc(v_mv1, 1)

            def normalise_block1(nth, dst, finished):
                dve.wait_ge(g_scales, nth)
                nc.vector.tensor_scalar(dst[:, 1], y1[:, 1], ln_rstd[:, 0, 1:2], ln_shift[:, 0, 1:2],
                                        ALU.mult, ALU.add).then_inc(finished, 1)

            degrees(0, LAST)
            low_t(0, LAST)
            add_x1(0, LAST - 2)
            low_v(0, LAST)
            low_x1(0, LAST - 1)
            for b in range(NB):
                dve.wait_ge(p_h, done(0, LAST) + b)
                nc.vector.tensor_tensor(y1[:, b], h_ps[:, b], bias[:], ALU.add).then_inc(v_hb, 1)
            dve.wait_ge(s_x[LAST % 2], landed(0, LAST))
            for b in range(NB):
                dve.wait_ge(v_hb, done(0, LAST) + b)
                nc.vector.scalar_tensor_tensor(y1[:, b], y1[:, b], 0.0, x[:, LAST % 2, b], ALU.max,
                                               ALU.add).then_inc(v_y1, 1)
            last_statistics(v_y1)
            low_b(0, LAST)
            low_g(0, LAST - 1)
            normalise_block1(1, x1[:, LAST % 2], v_x1)
            for b, bank_of in enumerate((ta_ps, tb_ps)):
                dve.wait_ge(a_x1t, done(0, LAST) + b)
                low(x1t_lo[:, b], bank_of[:, b], x1t_hi[:, b], v_x1t)
            add_x1(0, LAST - 1)
            low_g(0, LAST, v_ps)
            dve.wait_ge(g_x1, done(0, LAST))
            dve.wait_ge(v_x1, 1)
            for b in range(NB):
                dve.wait_ge(p_o, done(0, LAST) + b)
                nc.vector.scalar_tensor_tensor(y1[:, b], o_ps[:, b], 0.0, x1[:, LAST % 2, b], ALU.max,
                                               ALU.add).then_inc(v_y2, 1)
            last_statistics(v_y2)
            dve.wait_ge(s_res[LAST % 2], landed(0, LAST - 2))
            normalise_block1(2, res[:, LAST % 2], v_res)

        @block.tensor
        def _(pe):
            def product(dst, left, right, b, first, depth=range(2)):
                left_hi, left_lo = left
                right_hi, right_lo = right
                rows = slice(b * P, (b + 1) * P)
                for lh, rh in ((left_hi, right_lo), (left_lo, right_hi), (left_hi, right_hi)):
                    for kb in depth:
                        last = nc.tensor.matmul(dst, lh[:, kb, rows], rh[:, kb], start=first, stop=True,
                                                skip_group_check=True)
                        first = False
                return last

            def transposed(dst, src):
                for c in range(2):
                    for r in range(2):
                        last = nc.tensor.transpose(dst[:, c, r * P:(r + 1) * P], src[:, r, c * P:(c + 1) * P],
                                                   ident[:])
                return last

            def keep_clock(times):
                for _ in range(times):
                    nc.tensor.transpose(ta_ps[:, 0, 0:P], ident[:], ident[:])

            def u_product(base, c):
                if here(base, c):
                    pe.wait_ge(xt_split, done(base, c))
                    if here(base, c - 1):
                        pe.wait_ge(a_exp, done(base, c - 1))
                    for b in range(NB):
                        last = product(u_ps[:, b, 0:D + COLS], (xt_hi[:, c % 2], xt_lo[:, c % 2]), (w2_hi, w2_lo), b,
                                       True)
                    last.then_inc(p_u, 1)

            def broadcast_sj(base, c):
                if here(base, c):
                    if c == 0 and isinstance(base, int):
                        pe.wait_ge(v_scores, 1)
                    else:
                        pe.wait_ge(v_u, done(base, c))
                    for b in range(NB):
                        last = nc.tensor.transpose(sj_ps[:, b], scores[:, b, SJ:SJ + 1].broadcast_to([P, P]), ident[:])
                    last.then_inc(p_sj, 1)

            def transpose_b(base, c, b_bank=tb_ps):
                if here(base, c):
                    pe.wait_ge(g_badj, done(base, c))
                    transposed(b_bank, badj).then_inc(p_bt, 1)

            def transpose_t(base, c):
                if here(base, c):
                    pe.wait_ge(g_t, done(base, c))
                    if here(base, c - 1):
                        pe.wait_ge(v_bt, done(base, c - 1))
                    transposed(tb_ps, trans).then_inc(p_tt, 1)

            def vh_product(base, c):
                if here(base, c - 1):
                    pe.wait_ge(v_hb, done(base, c - 1))
                for b in range(NB):
                    product(vh_ps[:, b], (xt_hi[:, c % 2], xt_lo[:, c % 2]), (w10_hi, w10_lo), b, True)
                    if b == 0:
                        transpose_t(base, c)

            def tu_product(base, c):
                pe.wait_ge(v_tt, done(base, c))
                for b in range(NB):
                    last = product(v_ps[:, b], (tt_hi, tt_lo), (u_hi[:, c % 2], u_lo[:, c % 2]), b, False)
                last.then_inc(p_v, 1)

            def tv_product(base, c):
                pe.wait_ge(v_v, done(base, c))
                for b in range(NB):
                    last = product(h_ps[:, b], (tt_hi, tt_lo), (v_hi, v_lo), b, False)
                last.then_inc(p_h, 1)

            def transpose_x1(base, c):
                pe.wait_ge(g_x1, done(base, c))
                transposed(ta_ps, x1[:, c % 2]).then_inc(p_x1t, 1)

            def go_product(base, c):
                if here(base, c - 1):
                    pe.wait_ge(v_y2, done(base, c - 1))
                pe.wait_ge(v_x1t, done(base, c))
                for b in range(NB):
                    product(go_ps[:, b], (x1t_hi, x1t_lo), (wax_hi, wax_lo), b, True).then_inc(p_g, 1)

            def bg_product(base, c):
                pe.wait_ge(v_g, done_block(base, c, NB - 1))
                for b in range(NB):
                    last = product(o_ps[:, b], (bt_hi[:, c % 2], bt_lo[:, c % 2]), (g_hi, g_lo), b, False)
                last.then_inc(p_o, 1)

            def iteration(base, k):
                vh_product(base, k)
                u_product(base, k + 1)
                transpose_x1(base, k - 1)
                tu_product(base, k)
                broadcast_sj(base, k + 1)
                transpose_b(base, k)
                go_product(base, k - 1)
                tv_product(base, k)
                bg_product(base, k - 1)

            pe.wait_ge(s_ident, 1)
            keep_clock(CLOCK_TRANSPOSES[0])
            pe.wait_ge(s_x[0], 16)
            transposed(tb_ps, x[:, 0]).then_inc(p_xt, 1)
            keep_clock(CLOCK_TRANSPOSES[1])
            pe.wait_ge(xt_split, done(0, 0))
            pe.wait_ge(s_x[1], 16)
            transposed(tb_ps, x[:, 1]).then_inc(p_xt, 1)
            keep_clock(CLOCK_TRANSPOSES[2])
            pe.wait_ge(g_w, 1)
            pe.wait_ge(v_w, 1)
            u_product(0, 0)
            broadcast_sj(0, 0)
            pe.wait_ge(g_w, 3)
            product(vh_ps[:, 0], (xt_hi[:, 0], xt_lo[:, 0]), (w10_hi, w10_lo), 0, True)
            pe.wait_ge(v_u, done(0, 0))
            u_product(0, 1)
            product(vh_ps[:, 1], (xt_hi[:, 0], xt_lo[:, 0]), (w10_hi, w10_lo), 1, True).then_inc(p_vh0, 1)
            transpose_t(0, 0)
            broadcast_sj(0, 1)
            transpose_b(0, 0, ta_ps)
            pe.wait_ge(s_wcat, 16)
            transposed(g_ps, wcat[:, :, 0:D])
            transposed(o_ps, wcat[:, :, D:2 * D]).then_inc(s_wt, 1)
            tu_product(0, 0)
            u_product(0, 2)
            tv_product(0, 0)
            vh_product(0, 1)
            tu_product(0, 1)
            broadcast_sj(0, 2)
            transpose_b(0, 1)
            transpose_x1(0, 0)
            tv_product(0, 1)
            pe.wait_ge(v_w, 3)
            go_product(0, 0)
            bg_product(0, 0)
            with pe.Fori(0, LOOPED // UNROLL) as group:
                for k in range(FIRST_LOOPED, FIRST_LOOPED + UNROLL):
                    iteration(group * UNROLL, k)
            for k in AFTER:
                iteration(0, k)

            vh_product(0, LAST)
            tu_product(0, LAST)
            transpose_x1(0, LAST - 1)
            pe.wait_ge(v_v, done(0, LAST))
            for b in range(NB):
                product(h_ps[:, b], (tt_hi, tt_lo), (v_hi, v_lo), b, False).then_inc(p_h, 1)
            transpose_b(0, LAST)
            go_product(0, LAST - 1)
            pe.wait_ge(g_x1, done(0, LAST))
            pe.wait_ge(v_x1, 1)
            pe.wait_ge(v_bt, done(0, LAST))
            for b, bank_of in enumerate((ta_ps, tb_ps)):
                for r in range(NB):
                    last = nc.tensor.transpose(bank_of[:, b, r * P:(r + 1) * P],
                                               x1[:, LAST % 2, r, b * P:(b + 1) * P], ident[:])
                last.then_inc(p_x1t, 1)
            bg_product(0, LAST - 1)
            pe.wait_ge(v_hb, done(0, LAST) + NB - 1)
            for kb in range(DB):
                pe.wait_ge(v_x1t, done(0, LAST) + kb)
                for b in range(NB):
                    last = product(v_ps[:, b], (x1t_hi, x1t_lo), (wax_hi[:, :, 0:D], wax_lo[:, :, 0:D]), b, kb == 0, (kb,))
                    if kb == DB - 1:
                        last.then_inc(p_g, 1)
            pe.wait_ge(v_y2, done(0, LAST - 1))
            for b in range(NB):
                product(o_ps[:, b], (x1t_hi, x1t_lo), (wax_hi[:, :, D:2 * D], wax_lo[:, :, D:2 * D]), b, True)
            for kb in range(NB):
                pe.wait_ge(v_g, done_block(0, LAST, kb))
                for b in range(NB):
                    last = product(o_ps[:, b], (bt_hi[:, LAST % 2], bt_lo[:, LAST % 2]), (g_hi, g_lo), b, False, (kb,))
                    if kb == NB - 1:
                        last.then_inc(p_o, 1)


_INS = ["x", "adj", "L0_gnn_Wv", "L0_gnn_bv", "L0_gnn_aw", "L0_gnn_ab", "L0_gnn_Wk", "L0_gnn_bk", "L1_gnn_W"]


def kernel(**inputs):
    import numpy as np
    import concourse.bacc as bacc
    from concourse.bass_utils import run_bass_kernel_spmd

    nc = bacc.Bacc("TRN2", target_bir_lowering=False, num_devices=1)
    arrays, args = {}, []
    for name in _INS:
        a = np.ascontiguousarray(inputs[name])
        arrays[f"in_{name}"] = a
        args.append(nc.dram_tensor(f"in_{name}", a.shape, mybir.dt.from_np(a.dtype), kind="ExternalInput").ap())
    out = nc.dram_tensor("result", arrays["in_x"].shape, mybir.dt.float32, kind="ExternalOutput").ap()
    build(nc, *args, out)
    r = run_bass_kernel_spmd(nc, [arrays], core_ids=[0])
    return r.results[0]["result"]
```
